# Optimizing a Trainium2 kernel written in Bass

```python
import numpy as np
import jax
import jax.numpy as jnp

def _softmax(x, axis=-1):
    return jax.nn.softmax(x, axis=axis)

def _gelu(x):
    return jax.nn.gelu(x, approximate=True)

def _silu(x):
    return jax.nn.silu(x)

def _sigmoid(x):
    return jax.nn.sigmoid(x)

def _layernorm(x, axis=-1, eps=1e-05):
    m = jnp.mean(x, axis=axis, keepdims=True)
    v = jnp.var(x, axis=axis, keepdims=True)
    return (x - m) / jnp.sqrt(v + eps)

def _scatter_add(tgt, idx, src, axis=0):
    return tgt.at[idx].add(src)

def _segment_sum(src, seg, n):
    return jax.ops.segment_sum(src, seg, n)
kernel_name = 'mk_adaln_attn_ffn_d1_seqx_r8_fb44ea'

def setup_inputs(seed: int=0):
    np.random.seed(seed)
    _w = jnp.asarray

    def _rec_inputs():
        import jax
        import jax.numpy as jnp
        _rk = jax.random.key(seed)
        x = -0.000125 + 0.9999 * jax.random.normal(jax.random.fold_in(_rk, 1), (64, 32, 512), jnp.float32)
        _lenS = 32 - jax.random.randint(jax.random.fold_in(_rk, 7), (64,), 0, max(1, 32 // 4) + 1, jnp.int32)
        _lenS2 = 32 - jax.random.randint(jax.random.fold_in(_rk, 8), (64,), 0, max(1, 32 // 4) + 1, jnp.int32)
        cond_128 = 0.0061147 + 1.02565 * jax.random.normal(jax.random.fold_in(_rk, 11), (64, 128), jnp.float32)
        fside_S_0 = -0.022604 + 0.987366 * jax.random.normal(jax.random.fold_in(_rk, 12), (32,), jnp.float32)
        return (x, cond_128, fside_S_0)
    x, cond_128, fside_S_0 = _rec_inputs()

    def _L0_cond_setup():
        import jax, jax.numpy as jnp
        import numpy as np
        K = 8
        T = 1.0
        D_EMBD = 128
        IN_C = 32
        OUT_C = 32
        BS = 32
        H = 512
        HID = 128
        key = jax.random.key(seed)
        ks = jax.random.split(key, 10)
        s = lambda fan_in: 1.0 / np.sqrt(fan_in)
        return {'x': jax.random.normal(ks[0], (BS, IN_C, H), dtype=jnp.float32), 'embedding': jax.random.normal(ks[1], (BS, D_EMBD), dtype=jnp.float32), 'W0': jax.random.normal(ks[2], (D_EMBD, HID), dtype=jnp.float32) * s(D_EMBD), 'b0': jnp.zeros((HID,), dtype=jnp.float32), 'W1': jax.random.normal(ks[3], (HID, HID), dtype=jnp.float32) * s(HID), 'b1': jnp.zeros((HID,), dtype=jnp.float32), 'W2': jax.random.normal(ks[4], (HID, K), dtype=jnp.float32) * s(HID), 'b2': jnp.zeros((K,), dtype=jnp.float32), 'weight': jax.random.normal(ks[5], (K, OUT_C, IN_C, 1), dtype=jnp.float32) * s(IN_C), 'bias_k': jax.random.normal(ks[6], (K, OUT_C), dtype=jnp.float32) * 0.1}
    _L0_cond_all = _L0_cond_setup()
    _L0_cond_in = {k: v for k, v in _L0_cond_all.items() if k in ('W0', 'b0', 'W1', 'b1', 'W2', 'b2', 'weight', 'bias_k')}
    del _L0_cond_all

    def _L0_attn_setup():
        import jax, jax.numpy as jnp
        import numpy as np
        HIDDEN = 512
        NUM_HEADS = 32
        HEAD_DIM = HIDDEN // NUM_HEADS
        B, S = (2, 128)

        def _alibi_slopes(n):
            start = 2.0 ** (-2.0 ** (-(np.log2(n) - 3)))
            return np.array([start ** (i + 1) for i in range(n)], dtype=np.float32)
        key = jax.random.key(seed)
        k1, k2, k3, k4 = jax.random.split(key, 4)
        hidden_states = jax.random.normal(k1, (B, S, HIDDEN), jnp.float32)
        Wq = jax.random.normal(k2, (HIDDEN, HIDDEN), jnp.float32) * 0.02
        Wkv = jax.random.normal(k3, (HIDDEN, 2 * HEAD_DIM), jnp.float32) * 0.02
        Wo = jax.random.normal(k4, (HIDDEN, HIDDEN), jnp.float32) * 0.02
        return {'hidden_states': hidden_states, 'Wq': Wq, 'Wkv': Wkv, 'Wo': Wo}
    _L0_attn_all = _L0_attn_setup()
    _L0_attn_in = {k: v for k, v in _L0_attn_all.items() if k in ('Wq', 'Wkv', 'Wo')}
    del _L0_attn_all

    def _L0_cond2_setup():
        import jax, jax.numpy as jnp
        import numpy as np
        from jax import lax
        N, C_IN, L = (32, 32, 512)
        C_OUT, K, GROUPS = (32, 9, 4)
        C_DIM, PAD, STRIDE = (128, 4, 1)
        key = jax.random.key(seed)
        k1, k2, k3, k4, k5 = jax.random.split(key, 5)
        x = jax.random.normal(k1, (N, C_IN, L), dtype=jnp.float32)
        c = jax.random.normal(k2, (N, C_DIM), dtype=jnp.float32)
        weight = jax.random.normal(k3, (C_OUT, C_IN // GROUPS, K), dtype=jnp.float32)
        c_weight = jax.random.normal(k4, (C_OUT, C_DIM), dtype=jnp.float32)
        bias = jax.random.normal(k5, (C_OUT,), dtype=jnp.float32)
        return {'x': x, 'c': c, 'weight': weight, 'c_weight': c_weight, 'bias': bias}
    _L0_cond2_all = _L0_cond2_setup()
    _L0_cond2_in = {k: v for k, v in _L0_cond2_all.items() if k in ('weight', 'c_weight')}
    del _L0_cond2_all

    def _L0_ffn_setup():
        import jax, jax.numpy as jnp
        import numpy as np
        import math
        B, S, IN, OUT = (4, 256, 512, 512)
        E, R, K = (8, 64, 128)
        SCALE = 64.0 / 64.0
        MULTIPLIER = 1.0
        key = jax.random.key(seed)
        ks = jax.random.split(key, 6)
        return {'x': jax.random.normal(ks[0], (B, S, IN), jnp.float32), 'W_org': jax.random.normal(ks[1], (OUT, IN), jnp.float32) * 0.02, 'lora_down': jax.random.normal(ks[2], (E, IN, R), jnp.float32) * 0.02, 'lora_up': jax.random.normal(ks[3], (E, R, OUT), jnp.float32) * 0.02, 'lora_keys': jax.random.normal(ks[4], (E, K), jnp.float32), 'Wq': jax.random.normal(ks[5], (K, IN), jnp.float32) * 0.02}
    _L0_ffn_all = _L0_ffn_setup()
    _L0_ffn_in = {k: v for k, v in _L0_ffn_all.items() if k in ('W_org', 'lora_down', 'lora_up', 'lora_keys', 'Wq')}
    del _L0_ffn_all
    return {'x': x, 'cond_128': cond_128, 'fside_S_0': fside_S_0, 'L0_cond_W0': _L0_cond_in['W0'], 'L0_cond_b0': _L0_cond_in['b0'], 'L0_cond_W1': _L0_cond_in['W1'], 'L0_cond_b1': _L0_cond_in['b1'], 'L0_cond_W2': _L0_cond_in['W2'], 'L0_cond_b2': _L0_cond_in['b2'], 'L0_cond_weight': _L0_cond_in['weight'], 'L0_cond_bias_k': _L0_cond_in['bias_k'], 'L0_attn_Wq': _L0_attn_in['Wq'], 'L0_attn_Wkv': _L0_attn_in['Wkv'], 'L0_attn_Wo': _L0_attn_in['Wo'], 'L0_cond2_weight': _L0_cond2_in['weight'], 'L0_cond2_c_weight': _L0_cond2_in['c_weight'], 'L0_ffn_W_org': _L0_ffn_in['W_org'], 'L0_ffn_lora_down': _L0_ffn_in['lora_down'], 'L0_ffn_lora_up': _L0_ffn_in['lora_up'], 'L0_ffn_lora_keys': _L0_ffn_in['lora_keys'], 'L0_ffn_Wq': _L0_ffn_in['Wq']}

def reference(x, cond_128, fside_S_0, L0_cond_W0, L0_cond_b0, L0_cond_W1, L0_cond_b1, L0_cond_W2, L0_cond_b2, L0_cond_weight, L0_cond_bias_k, L0_attn_Wq, L0_attn_Wkv, L0_attn_Wo, L0_cond2_weight, L0_cond2_c_weight, L0_ffn_W_org, L0_ffn_lora_down, L0_ffn_lora_up, L0_ffn_lora_keys, L0_ffn_Wq):
    import jax
    import jax.numpy as jnp

    def _L0_cond_ref(x, embedding, W0, b0, W1, b1, W2, b2, weight, bias_k):
        import jax, jax.numpy as jnp
        import numpy as np
        K = 8
        T = 1.0
        D_EMBD = 128
        IN_C = 32
        OUT_C = 32
        BS = 32
        H = 512
        HID = 128
        h = jax.nn.gelu(embedding @ W0 + b0, approximate=False)
        h = jax.nn.gelu(h @ W1 + b1, approximate=False)
        att = jax.nn.softmax((h @ W2 + b2) / T, axis=-1)
        agg_w = jnp.einsum('bk,koi->boi', att, weight[..., 0])
        agg_b = att @ bias_k
        out = jnp.einsum('boi,bih->boh', agg_w, x) + agg_b[:, :, None]
        return out

    def _L0_attn_ref(hidden_states, Wq, Wkv, Wo):
        import jax, jax.numpy as jnp
        import numpy as np
        HIDDEN = 512
        NUM_HEADS = 32
        HEAD_DIM = HIDDEN // NUM_HEADS
        B, S = (2, 128)

        def _alibi_slopes(n):
            start = 2.0 ** (-2.0 ** (-(np.log2(n) - 3)))
            return np.array([start ** (i + 1) for i in range(n)], dtype=np.float32)
        b, s, h = hidden_states.shape
        scale = HEAD_DIM ** (-0.5)
        q = (hidden_states @ Wq).reshape(b, s, NUM_HEADS, HEAD_DIM)
        kv = hidden_states @ Wkv
        k, v = (kv[..., :HEAD_DIM], kv[..., HEAD_DIM:])
        scores = jnp.einsum('bqhd,bkd->bhqk', q, k) * scale
        pos = jnp.arange(s)
        slopes = jnp.asarray(_alibi_slopes(NUM_HEADS))
        bias = slopes[:, None, None] * (pos[None, None, :] - pos[None, :, None]).astype(jnp.float32)
        causal = pos[None, :] <= pos[:, None]
        scores = jnp.where(causal[None, None], scores + bias[None], -jnp.inf)
        attn = jax.nn.softmax(scores, axis=-1)
        out = jnp.einsum('bhqk,bkd->bqhd', attn, v).reshape(b, s, h)
        return out @ Wo

    def _L0_cond2_ref(x, c, weight, c_weight, bias):
        import jax, jax.numpy as jnp
        import numpy as np
        from jax import lax
        N, C_IN, L = (32, 32, 512)
        C_OUT, K, GROUPS = (32, 9, 4)
        C_DIM, PAD, STRIDE = (128, 4, 1)
        out = lax.conv_general_dilated(x, weight, window_strides=(STRIDE,), padding=[(PAD, PAD)], dimension_numbers=('NCH', 'OIH', 'NCH'), feature_group_count=GROUPS)
        ctx = jnp.einsum('nd,od->no', c, c_weight)
        out = out + ctx[:, :, None] + bias[None, :, None]
        return out

    def _L0_ffn_ref(x, W_org, lora_down, lora_up, lora_keys, Wq):
        import jax, jax.numpy as jnp
        import numpy as np
        import math
        B, S, IN, OUT = (4, 256, 512, 512)
        E, R, K = (8, 64, 128)
        SCALE = 64.0 / 64.0
        MULTIPLIER = 1.0
        base = jnp.einsum('bsi,oi->bso', x, W_org)
        q = jnp.einsum('bi,ki->bk', x.mean(axis=1), Wq)
        scores = jnp.einsum('bk,ek->be', q, lora_keys) / math.sqrt(K)
        coeffs = jax.nn.softmax(scores, axis=-1)
        h = jnp.einsum('bsi,eir->bser', x, lora_down)
        delta = jnp.einsum('be,bser,ero->bso', coeffs, h, lora_up)
        return base + delta * (SCALE * MULTIPLIER)
    x = x + _L0_attn_ref(_L0_cond_ref(x, cond_128, L0_cond_W0, L0_cond_b0, L0_cond_W1, L0_cond_b1, L0_cond_W2, L0_cond_b2, L0_cond_weight, L0_cond_bias_k), L0_attn_Wq, L0_attn_Wkv, L0_attn_Wo)
    x = x + _L0_ffn_ref(_L0_cond2_ref(x, cond_128, L0_cond2_weight, L0_cond2_c_weight, fside_S_0), L0_ffn_W_org, L0_ffn_lora_down, L0_ffn_lora_up, L0_ffn_lora_keys, L0_ffn_Wq)
    return x

_drawn_inputs = setup_inputs


def setup_inputs(seed=0):
    import zlib

    import numpy as np

    out = dict(_drawn_inputs(seed))
    spreads = {'L0_cond_b0': (0.0, 0.8), 'L0_cond_b1': (0.0, 2.0), 'L0_cond_b2': (0.0, 2.0)}
    factors = {'L0_cond_W0': 8.0,
     'L0_cond_W1': 8.0,
     'L0_cond_W2': 8.0,
     'L0_cond_weight': 2.714,
     'L0_cond_bias_k': 8.0,
     'L0_attn_Wq': 8.0,
     'L0_attn_Wkv': 2.918,
     'L0_attn_Wo': 2.903,
     'fside_S_0': 3.199}
    for name, (base, spread) in spreads.items():
        noise = np.random.default_rng([zlib.crc32(name.encode()), seed]).standard_normal(out[name].shape)
        drawn = base * np.exp(spread * noise) if base else spread * noise
        out[name] = jnp.asarray(drawn.astype(out[name].dtype))
    for name, factor in factors.items():
        out[name] = (out[name] * factor).astype(out[name].dtype)
    return out
```

```python
import concourse.bass as bass
from concourse import mybir
from contextlib import ExitStack

F32 = mybir.dt.float32
F32R = mybir.dt.float32r
ALU = mybir.AluOpType
ACT = mybir.ActivationFunctionType
AX = mybir.AxisListType

P = 128
BATCH, SEQ, DIM = 64, 32, 512
TOK = BATCH * SEQ
GROUPS = 8
GT = TOK // GROUPS
GB = GT // SEQ
NQ = GT // P
PH = DIM // P
HEADS, HD = 32, 16
HC = P // HD
PAIRS = GB // 2
EXPERTS, RANK = 8, 64
MIX = 8
HI, LO = 0, 1

START = dict(sel=128, qmask=16, condT=64, w0=128, w1=128, w2=8, b0=1, b1=1, b2=8, bank_bias=128, bank_w=256, kdiag=8,
             cwT=32, fside=32)
KEEP = dict(alibi=256, kvscale=1, quad=4, even=1, odd=1, keysT=8, wq2=512, ones=128)


def columns(pack):
    at, out = 0, {}
    for name, n in pack.items():
        out[name] = (at, at + n)
        at += n
    return out, at


START_AT, START_N = columns(START)
KEEP_AT, KEEP_N = columns(KEEP)
WEIGHTS = ["wq", "wo", "wd", "worg", "wu"]


def build(nc, x_d, start_d, keep_d, kvc_d, w_d, out_d):
    ctx = ExitStack()
    with ctx:
        def sb(name, shape, dt=F32):
            return ctx.enter_context(nc.sbuf_tensor(name, shape, dt))

        def sem(name):
            return ctx.enter_context(nc.semaphore(name))

        W = {n: sb(n, [P, 2, PH, DIM], F32R) for n in WEIGHTS}
        wkv = sb("wkv", [P, 2, PH, 4, 2 * HD], F32R)
        wconv = sb("wconv", [P, 2, 3, P], F32R)
        keep = sb("keep", [P, KEEP_N])
        c1_y = sb("c1_y", [P, 2, PH, GT], F32R)
        o_h = sb("o_h", [P, 2, PH, GT], F32R)
        q_x = sb("q_x", [P, 2, PH * GT], F32R)
        kdiag = sb("kdiag", [P, 2, HC, GT], F32R)
        vdiag = sb("vdiag", [P, 2 * GB * P + 64], F32R)
        probsT = sb("probsT", [P, 2, GB, HC, SEQ], F32R)
        xphase = sb("xphase", [P, 2, GB, P + 2], F32R)
        xin = sb("xin", [P, NQ * DIM])
        x1 = sb("x1", [P, NQ, DIM])
        tmp = sb("tmp", [P, 2, DIM])
        soft = sb("soft", [P, 5, DIM])
        aggb = sb("aggb", [P, TOK])
        ctxb = sb("ctxb", [P, TOK])
        mixd = sb("mixd", [P, 2, NQ, 4, SEQ], F32R)
        mix_att = sb("mix_att", [P, BATCH // 4, MIX])
        mix_a = sb("mix_a", [P, NQ, SEQ])
        mix_hl = sb("mix_hl", [P, 2, NQ, SEQ], F32R)
        smx = sb("smx", [P, PAIRS, 2 * HC])
        ssum = sb("ssum", [P, PAIRS, 2 * HC])
        srec = sb("srec", [P, PAIRS, 2 * HC])
        ysum = sb("ysum", [P, PH, GB])
        co = sb("co", [P, 4, GB * EXPERTS])
        comx = sb("comx", [P, 3, GB])
        coef = sb("coef", [P, 2, EXPERTS // 2, GB])
        attd = sb("attd", [P, BATCH // 4])
        mixs = sb("mixs", [P, 24])
        keep_bank = sb("keep_bank", [P, SEQ * MIX])
        hmlp = aggb[:, 0:2 * BATCH].rearrange("p (a b) -> p a b", a=2)
        diag_att = aggb[:, DIM:DIM + BATCH // 4 * MIX]
        start = soft[:, 3:5, :].rearrange("p a b -> p (a b)")

        def st(name):
            a, b = START_AT[name]
            return start[:, a:b]

        def kp(name):
            a, b = KEEP_AT[name]
            return keep[:, a:b]

        def q_half(s, k):
            return q_x[:, s, :].rearrange("p (b c s) -> p b c s", b=GB, c=PH)[:, :, 2 * k:2 * k + 2, :]

        ones = kp("ones")
        kvt = tmp[:, 0, 0:GT]
        kv_hl = soft[:, 3, :].bitcast(F32R).rearrange("p (s n) -> p s n", s=2)
        vnat = tmp[:, 1, :]
        kv_in = tmp[:, 0, 0:128].rearrange("p (t n) -> p t n", t=PH)

        bank = {n: ctx.enter_context(nc.psum_tensor(n, [P, DIM], F32))
                for n in ["feat0", "feat1", "sc0", "sc1", "row0", "row1", "conv", "small"]}
        feat = [bank["feat0"], bank["feat1"]]
        sc = [bank["sc0"], bank["sc1"]]
        row = [bank["row0"], bank["row1"]]
        ybank = [bank["conv"], bank["feat0"]]
        small = bank["small"]

        start_in, keep_in, kvc_in = sem("start_in"), sem("keep_in"), sem("kvc_in")
        stage_in = [sem(f"stage_in{u}") for u in range(3)]
        x_in, x1_in = sem("x_in"), [sem(f"x1_in{q}") for q in range(NQ)]
        k_spread = sem("k_spread")
        xph_in = [sem(f"xph_in{q}") for q in range(NQ)]
        out_done = [sem(f"out_done{q}") for q in range(NQ)]
        zeroed = sem("zeroed")
        w_hi, w_lo, kvc_hi, kvc_lo = sem("w_hi"), sem("w_lo"), sem("kvc_hi"), sem("kvc_lo")
        mlp_mm, mlp_act, mixs_dve, mixs_exp, bank_kept = (sem("mlp_mm"), sem("mlp_act"), sem("mixs_dve"),
                                                          sem("mixs_exp"), sem("bank_kept"))
        ctx_outer, ctx_mm, ctx_done = sem("ctx_outer"), sem("ctx_mm"), sem("ctx_done")
        agg_outer, agg_mm, agg_done = sem("agg_outer"), sem("agg_mm"), sem("agg_done")
        mix_prod, mix_red, mix_split, mix_ready = (sem("mix_prod"), sem("mix_red"), sem("mix_split"),
                                                   sem("mix_ready"))
        x_hi, x_lo = sem("x_hi"), sem("x_lo")
        c1_mm, c1_t, c1_hi, c1_lo = sem("c1_mm"), sem("c1_t"), sem("c1_hi"), sem("c1_lo")
        kv_mm, kv_t, kv_hi, kv_lo, v_tr, v_ready = (sem("kv_mm"), sem("kv_t"), sem("kv_hi"), sem("kv_lo"),
                                                    sem("v_tr"), sem("v_ready"))
        q_mm, q_hi, q_lo = sem("q_mm"), sem("q_hi"), sem("q_lo")
        s_mm, s_bias, s_max, s_sub, s_exp, s_sum, s_rec, s_norm, s_tr, p_hi, p_lo = (
            sem("s_mm"), sem("s_bias"), sem("s_max"), sem("s_sub"), sem("s_exp"), sem("s_sum"),
            sem("s_rec"), sem("s_norm"), sem("s_tr"), sem("p_hi"), sem("p_lo"))
        av_mm, o_hi, o_lo = sem("av_mm"), sem("o_hi"), sem("o_lo")
        wo_mm, x1_add = sem("wo_mm"), sem("x1_add")
        xph_hi, xph_lo = sem("xph_hi"), sem("xph_lo")
        y_mm, y_t, y_sum, y_hi, y_lo = sem("y_mm"), sem("y_t"), sem("y_sum"), sem("y_hi"), sem("y_lo")
        co_mm, co_dve, co_exp = sem("co_mm"), sem("co_dve"), sem("co_exp")
        h_mm, h_t, h_hi, h_lo = sem("h_mm"), sem("h_t"), sem("h_hi"), sem("h_lo")
        out_mm, out_add = sem("out_mm"), sem("out_add")

        x_g = x_d.rearrange("(g q p) c -> p g q c", q=NQ, p=P)
        out_g = out_d.rearrange("(g q p) c -> p g q c", q=NQ, p=P)

        NW = len(WEIGHTS) * PH
        EARLY = 12

        def slot_of(n):
            return n % 3 if n < EARLY else n % 2

        def stage(n):
            u = slot_of(n)
            return soft[:, 2, :] if u == 2 else x1[:, u, :]

        def stage_count(n):
            return sum(1 for m in range(n + 1) if slot_of(m) == slot_of(n))

        NB4 = BATCH // 4
        CO = 9

        block = ctx.enter_context(nc.Block())

        @block.sync
        def _(sp):
            sp.dma_start(start[:, 0:START_N], start_d).then_inc(start_in, 16)
            sp.dma_start(xin[:].rearrange("p (q c) -> p q c", q=NQ), x_g[:, 0]).then_inc(x_in, 16)
            sp.dma_start(keep[:], keep_d).then_inc(keep_in, 16)
            sp.dma_start(tmp[:, 0, :], kvc_d).then_inc(kvc_in, 16)

            def load_weight(n):
                prev = [m for m in range(n) if slot_of(m) == slot_of(n)]
                if prev:
                    sp.wait_ge(w_hi, prev[-1] + 1)
                    sp.wait_ge(w_lo, prev[-1] + 1)
                name, c = WEIGHTS[n // PH], n % PH
                sp.dma_start(stage(n), w_d[name][:, c * DIM:(c + 1) * DIM]).then_inc(stage_in[slot_of(n)], 16)

            def spread_k(g):
                if type(g) is int and g == 0:
                    sp.wait_ge(zeroed, 3)
                sp.wait_ge(kv_hi, g + 1)
                sp.wait_ge(kv_lo, g + 1)
                for h in range(HC):
                    src = 32 * (h % 4)
                    sp.dma_start(kdiag[HD * h:HD * (h + 1), :, h, :].bitcast(F32),
                                 kv_hl[src:src + HD, :, :].bitcast(F32)).then_inc(k_spread, 16)

            def load_x(g):
                sp.dma_start(xin[:].rearrange("p (q c) -> p q c", q=NQ),
                             x_g[:, bass.ds(g, 1)].squeeze(1)).then_inc(x_in, 16)

            def load_x1(g, q):
                sp.dma_start(x1[:, q, :], x_g[:, bass.ds(g, 1), q].squeeze(1)).then_inc(x1_in[q], 16)

            def by_phase(b):
                for q in range(NQ):
                    sp.wait_ge(x1_add, NQ * b + q + 1)
                    for m in range(4):
                        for t in range(PH):
                            at = (4 * q + m) * P
                            sp.dma_start(xin[32 * t:32 * t + 32, at:at + P],
                                         x1[32 * m:32 * m + 32, q, t * P:(t + 1) * P]).then_inc(xph_in[q], 16)

            def store(b, last):
                for q in range(NQ):
                    sp.wait_ge(out_add, NQ * b + q + 1)
                    sp.dma_start(out_g[:, bass.ds(b, 1), q].squeeze(1), x1[:, q, :]).then_inc(out_done[q], 16)
                for q in range(NQ):
                    sp.wait_ge(out_done[q], 16 * (b + 1))
                    if not last:
                        load_x1(b + 1, q)

            for n in range(NW):
                load_weight(n)
                if n == 11:
                    spread_k(0)
                    sp.wait_ge(x_hi, 1)
                    sp.wait_ge(x_lo, NQ)
                    load_x(1)
            sp.wait_ge(w_hi, NW)
            sp.wait_ge(w_lo, NW)
            for q in range(NQ):
                load_x1(0, q)

            with sp.Fori(1, GROUPS - 1) as g:
                by_phase(g - 1)
                spread_k(g)
                sp.wait_ge(xph_hi, NQ * g)
                sp.wait_ge(xph_lo, NQ * g)
                load_x(g + 1)
                store(g - 1, False)
            by_phase(GROUPS - 2)
            spread_k(GROUPS - 1)
            store(GROUPS - 2, False)
            by_phase(GROUPS - 1)
            store(GROUPS - 1, True)

        @block.tensor
        def _(pe):
            def split_mm(out, a_hi, a_lo, b_hi, b_lo, first, last):
                pe.matmul(out, a_hi, b_hi, start=first, stop=False)
                pe.matmul(out, a_hi, b_lo, start=False, stop=False)
                return pe.matmul(out, a_lo, b_hi, start=False, stop=last)

            pe.wait_ge(zeroed, 3)

            def ctx_part(c):
                pe.wait_ge(ctx_outer, c + 1)
                pe.matmul(sc[c % 2][:], ones, soft[:, c % 2, :], start=True, stop=True).then_inc(ctx_mm, 1)

            pe.wait_ge(start_in, 16)
            pe.matmul(small[:, 0:BATCH], st("w0"), st("condT"), start=True, stop=True).then_inc(mlp_mm, 1)
            pe.wait_ge(keep_in, 16)
            ctx_part(0)
            ctx_part(1)
            pe.wait_ge(mlp_act, 1)
            pe.matmul(small[:, 0:BATCH], st("w1"), hmlp[:, 0, :], start=True, stop=True).then_inc(mlp_mm, 1)
            pe.wait_ge(mlp_act, 2)
            pe.matmul(small[0:BATCH, 0:MIX], hmlp[:, 1, :], st("w2"), start=True, stop=True).then_inc(mlp_mm, 1)
            for c in range(2, 4):
                pe.wait_ge(ctx_done, c - 1)
                ctx_part(c)

            pe.wait_ge(mixs_dve, 7)
            pe.matmul(small[:, 0:NB4 * MIX], st("sel")[0:BATCH, :], diag_att[0:BATCH, :],
                      start=True, stop=True).then_inc(mlp_mm, 1)

            def agg_part(c):
                pe.wait_ge(agg_outer, c + 1)
                pe.wait_ge(ctx_done, 3 + c % 2)
                if c >= 2:
                    pe.wait_ge(agg_done, c - 1)
                pe.matmul(sc[c % 2][:], ones, soft[:, c % 2, :], start=True, stop=True).then_inc(agg_mm, 1)

            def mix(g):
                pe.wait_ge(x_hi, g + 1)
                pe.wait_ge(x_lo, NQ * (g + 1))
                pe.wait_ge(mix_ready, g + 1)
                for k in range(2):
                    for t in range(2 * k, 2 * k + 2):
                        for q in range(NQ):
                            at = (t % 2) * GT + q * P
                            xs = [q_x[:, s, q * DIM + t * P:q * DIM + (t + 1) * P] for s in (HI, LO)]
                            ms = [mixd[:, s, q].rearrange("p a b -> p (a b)") for s in (HI, LO)]
                            mm = split_mm(feat[k][:, at:at + P], xs[HI], xs[LO], ms[HI], ms[LO], True, True)
                    mm.then_inc(c1_mm, 1)

            def kv_and_q(g):
                pe.wait_ge(kvc_hi, 1)
                pe.wait_ge(kvc_lo, 1)
                for t in range(PH):
                    if t % 2 == 0:
                        pe.wait_ge(c1_hi, 2 * g + t // 2 + 1)
                        pe.wait_ge(c1_lo, 2 * g + t // 2 + 1)
                    ws = [wkv[:, s, t].rearrange("p r n -> p (r n)") for s in (HI, LO)]
                    mm = split_mm(small[:, 0:GT], ws[HI], ws[LO], c1_y[:, HI, t, :], c1_y[:, LO, t, :],
                                  t == 0, t == PH - 1)
                mm.then_inc(kv_mm, 1)
                pe.wait_ge(w_hi, PH)
                pe.wait_ge(w_lo, PH)
                for c in range(PH):
                    for t in range(PH):
                        ws = [W["wq"][:, s, t, c * P:(c + 1) * P] for s in (HI, LO)]
                        at = (c % 2) * GT
                        mm = split_mm(feat[c // 2][:, at:at + GT], ws[HI], ws[LO],
                                      c1_y[:, HI, t, :], c1_y[:, LO, t, :], t == 0, t == PH - 1)
                    if c % 2:
                        mm.then_inc(q_mm, 1)

            def scores(g, p):
                if p == 0:
                    pe.wait_ge(q_hi, 2 * (g + 1))
                    pe.wait_ge(q_lo, 2 * (g + 1))
                    pe.wait_ge(k_spread, 16 * HC * (g + 1))
                if p >= 2:
                    pe.wait_ge(s_bias, PAIRS * g + p - 1)
                for b in (2 * p, 2 * p + 1):
                    qs = [q_x[:, s, b * P:(b + 1) * P] for s in (HI, LO)]
                    ks = [kdiag[:, s, :, b * SEQ:(b + 1) * SEQ] for s in (HI, LO)]
                    at = (b % 2) * GT
                    mm = split_mm(sc[p % 2][:, at:at + GT], qs[HI], qs[LO], ks[HI], ks[LO], True, True)
                mm.then_inc(s_mm, 1)

            def attend(b):
                pe.wait_ge(v_ready, b + 1)
                for q in range(NQ):
                    pe.wait_ge(p_hi, PAIRS * b + 2 * q + 2)
                    pe.wait_ge(p_lo, PAIRS * b + 2 * q + 2)
                    for m in range(4):
                        n = 4 * q + m
                        for half in range(2):
                            vs = []
                            for s in (HI, LO):
                                at = (s * GB + n) * P + (64 if half == 0 else 0)
                                vs.append(vdiag[:, at:at + P])
                            ps = [probsT[:, s, n, 4 * half:4 * half + 4, :].rearrange("p a b -> p (a b)")
                                  for s in (HI, LO)]
                            mm = split_mm(sc[q][:, m * P:(m + 1) * P], vs[HI], vs[LO], ps[HI], ps[LO],
                                          half == 0, half == 1)
                    mm.then_inc(av_mm, 1)

            def out_proj(b):
                pe.wait_ge(w_hi, 2 * PH)
                pe.wait_ge(w_lo, 2 * PH)
                for q in range(NQ):
                    pe.wait_ge(o_hi, NQ * b + q + 1)
                    pe.wait_ge(o_lo, NQ * b + q + 1)
                    for c in range(PH):
                        os = [o_h[:, s, c, q * P:(q + 1) * P] for s in (HI, LO)]
                        mm = split_mm(row[q][:], os[HI], os[LO], W["wo"][:, HI, c, :], W["wo"][:, LO, c, :],
                                      c == 0, c == PH - 1)
                    mm.then_inc(wo_mm, 1)

            def conv(b, with_front):
                for q in range(NQ):
                    pe.wait_ge(xph_hi, NQ * b + q + 1)
                    pe.wait_ge(xph_lo, NQ * b + q + 1)
                    if q == 1 and with_front:
                        pe.wait_ge(q_hi, 2 * (b + 1) + 1)
                        pe.wait_ge(q_lo, 2 * (b + 1) + 1)
                    for m in range(4):
                        n = 4 * q + m
                        for k in range(3):
                            xs = [xphase[:, s, n, k:k + P] for s in (HI, LO)]
                            mm = split_mm(ybank[q][:, m * P:(m + 1) * P], xs[HI], xs[LO],
                                          wconv[:, HI, k, :], wconv[:, LO, k, :], k == 0, k == 2)
                    mm.then_inc(y_mm, 1)

            def coef_query(b):
                pe.wait_ge(y_sum, NQ * (b + 1))
                for t in range(PH):
                    mm = pe.matmul(small[:, 0:GB], kp("wq2")[:, t * P:(t + 1) * P], ysum[:, t, :],
                                   start=(t == 0), stop=(t == PH - 1))
                mm.then_inc(co_mm, 1)

            def coef_scores(b):
                pe.wait_ge(co_dve, CO * b + 2)
                pe.matmul(small[:, 64:64 + GB * EXPERTS], ones, co[:, 1, :], start=True, stop=True)\
                  .then_inc(co_mm, 1)

            def lora_down(b, k):
                pe.wait_ge(w_hi, 3 * PH)
                pe.wait_ge(w_lo, 3 * PH)
                pe.wait_ge(y_hi, NQ * (b + 1))
                pe.wait_ge(y_lo, NQ * (b + 1))
                for e in (2 * k, 2 * k + 1):
                    for t in range(PH):
                        ws = [W["wd"][:, s, t, e * P:(e + 1) * P] for s in (HI, LO)]
                        at = (e % 2) * GT
                        mm = split_mm(feat[k][:, at:at + GT], ws[HI], ws[LO],
                                      c1_y[:, HI, t, :], c1_y[:, LO, t, :], t == 0, t == PH - 1)
                mm.then_inc(h_mm, 1)

            def base(q):
                if q == 0:
                    pe.wait_ge(w_hi, 4 * PH)
                    pe.wait_ge(w_lo, 4 * PH)
                for t in range(PH):
                    ys = [c1_y[:, s, t, q * P:(q + 1) * P] for s in (HI, LO)]
                    split_mm(row[q][:], ys[HI], ys[LO], W["worg"][:, HI, t, :], W["worg"][:, LO, t, :],
                             t == 0, False)

            def lora_up(b):
                pe.wait_ge(w_hi, 5 * PH)
                pe.wait_ge(w_lo, 5 * PH)
                pe.wait_ge(h_hi, 2 * (b + 1))
                pe.wait_ge(h_lo, 2 * (b + 1))
                for q in range(NQ):
                    for e in range(PH):
                        hs = [o_h[:, s, e, q * P:(q + 1) * P] for s in (HI, LO)]
                        mm = split_mm(row[q][:], hs[HI], hs[LO], W["wu"][:, HI, e, :], W["wu"][:, LO, e, :],
                                      False, e == PH - 1)
                    mm.then_inc(out_mm, 1)

            agg_part(0)
            mix(0)
            for c in range(1, 4):
                agg_part(c)
            kv_and_q(0)
            for p in range(PAIRS):
                if p == 0:
                    pe.wait_ge(agg_done, 4)
                scores(0, p)

            with pe.Fori(1, GROUPS) as g:
                attend(g - 1)
                mix(g)
                out_proj(g - 1)
                kv_and_q(g)
                conv(g - 1, True)
                scores(g, 0)
                scores(g, 1)
                coef_query(g - 1)
                lora_down(g - 1, 0)
                coef_scores(g - 1)
                scores(g, 2)
                lora_down(g - 1, 1)
                scores(g, 3)
                base(0)
                base(1)
                lora_up(g - 1)
            b = GROUPS - 1
            attend(b)
            out_proj(b)
            conv(b, False)
            coef_query(b)
            lora_down(b, 0)
            coef_scores(b)
            lora_down(b, 1)
            base(0)
            base(1)
            lora_up(b)

        @block.scalar
        def _(act):
            def copy(out, in_):
                return act.activation(out, in_, ACT.Copy)

            act.wait_ge(mlp_mm, 1)
            act.activation(hmlp[:, 0, :], small[:, 0:BATCH], ACT.Gelu, bias=st("b0")).then_inc(mlp_act, 1)
            act.wait_ge(mlp_mm, 2)
            act.activation(hmlp[:, 1, :], small[:, 0:BATCH], ACT.Gelu, bias=st("b1")).then_inc(mlp_act, 1)

            def split_weight(n):
                act.wait_ge(stage_in[slot_of(n)], 16 * stage_count(n))
                copy(W[WEIGHTS[n // PH]][:, HI, n % PH, :], stage(n)).then_inc(w_hi, 1)

            def x_split(g):
                act.wait_ge(x_in, 16 * (g + 1))
                copy(q_x[:, HI, :], xin[:]).then_inc(x_hi, 1)

            def aggb_copy(c):
                act.wait_ge(agg_mm, c + 1)
                copy(aggb[:, c * DIM:(c + 1) * DIM], sc[c % 2][:]).then_inc(agg_done, 1)

            def c1_split(g):
                for k in range(2):
                    act.wait_ge(c1_t, 2 * g + k + 1)
                    copy(c1_y[:, HI, 2 * k:2 * k + 2, :].rearrange("p a b -> p (a b)"),
                         tmp[:, k, :]).then_inc(c1_hi, 1)

            def kvq_split(g):
                act.wait_ge(kv_t, g + 1)
                copy(kv_hl[:, HI, :], kvt).then_inc(kv_hi, 1)
                for k in range(2):
                    act.wait_ge(q_mm, 2 * g + k + 1)
                    copy(q_half(HI, k), feat[k][:].rearrange("p (c b s) -> p b c s", c=2, b=GB)).then_inc(q_hi, 1)

            def exp(g, p):
                act.wait_ge(s_sub, PAIRS * g + p + 1)
                act.activation(soft[:, p % 3, :], soft[:, p % 3, :], ACT.Exp).then_inc(s_exp, 1)

            def probs_split(g, p):
                act.wait_ge(s_tr, PAIRS * g + p + 1)
                copy(probsT[:, HI, 2 * p:2 * p + 2].rearrange("p a b c -> p (a b c)"),
                     soft[:, 3 + p % 2, :]).then_inc(p_hi, 1)

            def o_split(b):
                for q in range(NQ):
                    act.wait_ge(av_mm, NQ * b + q + 1)
                    copy(o_h[:, HI, :, q * P:(q + 1) * P].rearrange("p h (b s) -> p b h s", b=4),
                         sc[q][:].rearrange("p (b h s) -> p b h s", b=4, h=4)).then_inc(o_hi, 1)

            def xph_split(b):
                for q in range(NQ):
                    act.wait_ge(xph_in[q], 16 * 4 * PH * (b + 1))
                    copy(xphase[:, HI, 4 * q:4 * q + 4, 1:P + 1],
                         xin[:, q * DIM:(q + 1) * DIM].rearrange("p (b j) -> p b j", b=4)).then_inc(xph_hi, 1)

            def y_split(b):
                for q in range(NQ):
                    act.wait_ge(y_t, NQ * b + q + 1)
                    copy(c1_y[:, HI, :, q * P:(q + 1) * P],
                         tmp[:, q, :].rearrange("p (t n) -> p t n", t=PH)).then_inc(y_hi, 1)

            def coef_exp(b):
                act.wait_ge(co_dve, CO * b + 4)
                act.activation(co[:, 3, :], co[:, 2, :], ACT.Exp,
                               scale=1.0 / (SEQ * 128.0 ** 0.5)).then_inc(co_exp, 1)

            def h_split(b):
                for k in range(2):
                    act.wait_ge(h_t, 2 * b + k + 1)
                    copy(o_h[:, HI, 2 * k:2 * k + 2, :].rearrange("p a b -> p (a b)"),
                         tmp[:, k, :]).then_inc(h_hi, 1)

            act.wait_ge(kvc_in, 16)
            copy(wkv[:, HI], kv_in.unsqueeze(2).to_broadcast((P, PH, 4, 2 * HD)))
            copy(wconv[:, HI].rearrange("p a b -> p (a b)"), tmp[:, 0, 128:512]).then_inc(kvc_hi, 1)
            x_split(0)
            for n in range(3):
                split_weight(n)
            act.wait_ge(mixs_dve, 3)
            act.activation(mixs[0:BATCH, 8:8 + MIX], mixs[0:BATCH, 0:MIX], ACT.Exp).then_inc(mixs_exp, 1)
            split_weight(3)
            aggb_copy(0)
            c1_split(0)
            for n in range(PH, 2 * PH):
                split_weight(n)
            for c in range(1, 4):
                aggb_copy(c)
            kvq_split(0)
            for n in range(2 * PH, EARLY):
                split_weight(n)
            exp(0, 0)
            exp(0, 1)
            exp(0, 2)
            probs_split(0, 0)
            exp(0, 3)
            probs_split(0, 1)
            probs_split(0, 2)
            probs_split(0, 3)
            for n in range(EARLY, NW):
                split_weight(n)
            act.wait_ge(s_mm, PAIRS)
            x_split(1)

            with act.Fori(1, GROUPS - 1) as g:
                o_split(g - 1)
                c1_split(g)
                kvq_split(g)
                xph_split(g - 1)
                y_split(g - 1)
                exp(g, 0)
                exp(g, 1)
                coef_exp(g - 1)
                exp(g, 2)
                probs_split(g, 0)
                h_split(g - 1)
                exp(g, 3)
                probs_split(g, 1)
                probs_split(g, 2)
                probs_split(g, 3)
                x_split(g + 1)
            g = GROUPS - 1
            o_split(g - 1)
            c1_split(g)
            kvq_split(g)
            xph_split(g - 1)
            y_split(g - 1)
            exp(g, 0)
            exp(g, 1)
            coef_exp(g - 1)
            exp(g, 2)
            probs_split(g, 0)
            h_split(g - 1)
            exp(g, 3)
            probs_split(g, 1)
            probs_split(g, 2)
            probs_split(g, 3)
            o_split(g)
            xph_split(g)
            y_split(g)
            coef_exp(g)
            h_split(g)

        @block.gpsimd
        def _(pool):
            def lo_of(out, whole, hi):
                return pool.tensor_tensor(out, whole, hi.bitcast(F32), ALU.subtract)

            pool.memset(kdiag[:].bitcast(F32).rearrange("p a b c -> p (a b c)"), 0.0).then_inc(zeroed, 1)
            pool.memset(vdiag[:].bitcast(F32), 0.0).then_inc(zeroed, 1)
            pool.memset(xphase[:, :, :, 0:P + 2:P + 1].bitcast(F32), 0.0).then_inc(zeroed, 1)

            def split_weight(n):
                pool.wait_ge(w_hi, n + 1)
                pool.wait_ge(w_lo, n)
                w = W[WEIGHTS[n // PH]]
                lo_of(w[:, LO, n % PH, :], stage(n), w[:, HI, n % PH, :]).then_inc(w_lo, 1)

            def x_split(g):
                pool.wait_ge(x_hi, g + 1)
                for q in range(NQ):
                    sl = slice(q * DIM, (q + 1) * DIM)
                    lo_of(q_x[:, LO, sl], xin[:, sl], q_x[:, HI, sl]).then_inc(x_lo, 1)

            def mix_product(g):
                for q in range(NQ):
                    last = pool.tensor_tensor(
                        soft[:, 1, q * 256:(q + 1) * 256].rearrange("p (o k) -> p o k", k=MIX),
                        mix_att[:, bass.ds(NQ * g + q, 1), :].to_broadcast((P, SEQ, MIX)),
                        keep_bank[:].rearrange("p (o k) -> p o k", k=MIX), ALU.mult)
                return last

            def mix_diag(g):
                pool.wait_ge(mix_split, 2 * (g + 1))
                pool.tensor_tensor(
                    mixd[:].rearrange("p s q m o -> p (s q) m o"),
                    mix_hl[:].bitcast(F32).rearrange("p s q o -> p (s q) o").unsqueeze(2)
                    .to_broadcast((P, 2 * NQ, 4, SEQ)),
                    kp("quad").unsqueeze(1).unsqueeze(3).to_broadcast((P, 2 * NQ, 4, SEQ)),
                    ALU.mult).then_inc(mix_ready, 1)

            def c1_split(g):
                for k in range(2):
                    pool.wait_ge(c1_hi, 2 * g + k + 1)
                    sl = [c1_y[:, s, 2 * k:2 * k + 2, :].rearrange("p a b -> p (a b)") for s in (HI, LO)]
                    lo_of(sl[LO], tmp[:, k, :], sl[HI]).then_inc(c1_lo, 1)

            def v_spread(g):
                pool.wait_ge(zeroed, 3)
                pool.wait_ge(v_tr, g + 1)
                pool.tensor_tensor(
                    vdiag[:, 0:2 * GB * P].rearrange("p (n z c d) -> p n z c d", z=2, c=4, d=HD)[:, :, 1],
                    vnat.rearrange("p (n e) -> p n e", e=2 * HD)[:, :, HD:2 * HD].unsqueeze(2)
                    .to_broadcast((P, 2 * GB, 4, HD)),
                    kp("quad").unsqueeze(1).unsqueeze(3).to_broadcast((P, 2 * GB, 4, HD)),
                    ALU.mult).then_inc(v_ready, 1)

            def heads(ap):
                return ap.rearrange("p (h k) -> p h k", k=SEQ)

            def s_subtract(g, p):
                pool.wait_ge(s_max, PAIRS * g + p + 1)
                s = heads(soft[:, p % 3, :])
                pool.tensor_tensor(s, s, smx[:, p, :].unsqueeze(2).to_broadcast((P, 2 * HC, SEQ)),
                                   ALU.subtract).then_inc(s_sub, 1)

            def s_normalize(g, p):
                pool.wait_ge(s_rec, PAIRS * g + p + 1)
                s = heads(soft[:, p % 3, :])
                pool.tensor_tensor(s, s, srec[:, p, :].unsqueeze(2).to_broadcast((P, 2 * HC, SEQ)),
                                   ALU.mult).then_inc(s_norm, 1)

            def xph_split(b):
                for q in range(NQ):
                    pool.wait_ge(xph_hi, NQ * b + q + 1)
                    lo_of(xphase[:, LO, 4 * q:4 * q + 4, 1:P + 1],
                          xin[:, q * DIM:(q + 1) * DIM].rearrange("p (b j) -> p b j", b=4),
                          xphase[:, HI, 4 * q:4 * q + 4, 1:P + 1]).then_inc(xph_lo, 1)

            def y_split(b):
                for q in range(NQ):
                    pool.wait_ge(y_hi, NQ * b + q + 1)
                    lo_of(c1_y[:, LO, :, q * P:(q + 1) * P],
                          tmp[:, q, :].rearrange("p (t n) -> p t n", t=PH),
                          c1_y[:, HI, :, q * P:(q + 1) * P]).then_inc(y_lo, 1)

            def h_split(b):
                for k in range(2):
                    pool.wait_ge(h_hi, 2 * b + k + 1)
                    sl = [o_h[:, s, 2 * k:2 * k + 2, :].rearrange("p a b -> p (a b)") for s in (HI, LO)]
                    lo_of(sl[LO], tmp[:, k, :], sl[HI]).then_inc(h_lo, 1)

            pool.wait_ge(kvc_hi, 1)
            lo_of(wkv[:, LO], kv_in.unsqueeze(2).to_broadcast((P, PH, 4, 2 * HD)), wkv[:, HI])
            lo_of(wconv[:, LO].rearrange("p a b -> p (a b)"), tmp[:, 0, 128:512],
                  wconv[:, HI].rearrange("p a b -> p (a b)")).then_inc(kvc_lo, 1)
            x_split(0)
            for c in range(4):
                pool.wait_ge(mixs_dve, 10)
                pool.wait_ge(mix_red, 1)
                if c >= 2:
                    pool.wait_ge(agg_mm, c - 1)
                pool.tensor_tensor(
                    soft[:, c % 2, :].rearrange("p (q n) -> p q n", q=4),
                    attd[:, 4 * c:4 * c + 4].unsqueeze(2).to_broadcast((P, 4, P)),
                    st("bank_bias").unsqueeze(1).to_broadcast((P, 4, P)), ALU.mult).then_inc(agg_outer, 1)
                if c == 0:
                    mix_diag(0)
            c1_split(0)
            for n in range(PH, 2 * PH):
                split_weight(n)
            v_spread(0)
            for n in range(2 * PH, EARLY):
                split_weight(n)
            s_subtract(0, 0)
            s_subtract(0, 1)
            s_normalize(0, 0)
            s_subtract(0, 2)
            s_normalize(0, 1)
            s_subtract(0, 3)
            s_normalize(0, 2)
            s_normalize(0, 3)
            pool.wait_ge(s_tr, 2)
            mix_product(1).then_inc(mix_prod, 1)
            for n in range(EARLY, NW):
                split_weight(n)
            x_split(1)
            mix_diag(1)

            def body(g, last):
                c1_split(g)
                v_spread(g)
                xph_split(g - 1)
                y_split(g - 1)
                s_subtract(g, 0)
                s_subtract(g, 1)
                s_normalize(g, 0)
                s_subtract(g, 2)
                s_normalize(g, 1)
                h_split(g - 1)
                s_subtract(g, 3)
                s_normalize(g, 2)
                s_normalize(g, 3)
                if not last:
                    pool.wait_ge(s_tr, PAIRS * g + 2)
                    mix_product(g + 1).then_inc(mix_prod, 1)
                    x_split(g + 1)
                    mix_diag(g + 1)

            with pool.Fori(1, GROUPS - 1) as g:
                body(g, False)
            body(GROUPS - 1, True)
            b = GROUPS - 1
            xph_split(b)
            y_split(b)
            h_split(b)

        @block.vector
        def _(dve):
            add, sub, mult = ALU.add, ALU.subtract, ALU.mult

            def heads(ap):
                return ap.rearrange("p (h k) -> p h k", k=SEQ)

            def ctx_outer_product(c):
                if c >= 2:
                    dve.wait_ge(ctx_mm, c - 1)
                dve.tensor_tensor(soft[:, c % 2, :].rearrange("p (b o) -> p b o", o=SEQ),
                                  st("condT")[:, 16 * c:16 * c + 16].unsqueeze(2).to_broadcast((P, 16, SEQ)),
                                  st("cwT").unsqueeze(1).to_broadcast((P, 16, SEQ)), mult)\
                   .then_inc(ctx_outer, 1)

            def ctx_add_bias(c):
                dve.wait_ge(ctx_mm, c + 1)
                dve.tensor_tensor(ctxb[:, c * DIM:(c + 1) * DIM].rearrange("p (b o) -> p b o", o=SEQ),
                                  sc[c % 2][:].rearrange("p (b o) -> p b o", o=SEQ),
                                  st("fside").unsqueeze(1).to_broadcast((P, 16, SEQ)), add)\
                   .then_inc(ctx_done, 1)

            def split_weight(n):
                dve.wait_ge(w_hi, n + 1)
                w = W[WEIGHTS[n // PH]]
                dve.tensor_tensor(w[:, LO, n % PH, :], stage(n), w[:, HI, n % PH, :].bitcast(F32), sub)\
                   .then_inc(w_lo, 1)

            dve.wait_ge(start_in, 16)
            ctx_outer_product(0)
            ctx_outer_product(1)
            dve.tensor_copy(keep_bank[:], st("bank_w")).then_inc(bank_kept, 1)
            ctx_add_bias(0)
            ctx_add_bias(1)
            ctx_outer_product(2)
            ctx_outer_product(3)
            split_weight(0)
            split_weight(1)
            lg, B = mixs[0:BATCH], BATCH
            dve.wait_ge(mlp_mm, 3)
            dve.tensor_tensor(lg[:, 0:MIX], small[0:B, 0:MIX], st("b2")[0:B, :], add).then_inc(mixs_dve, 1)
            dve.wait_ge(mixs_dve, 1)
            dve.tensor_reduce(lg[:, 16:17], lg[:, 0:MIX], AX.X, ALU.max).then_inc(mixs_dve, 1)
            dve.wait_ge(mixs_dve, 2)
            dve.tensor_scalar(lg[:, 0:MIX], lg[:, 0:MIX], lg[:, 16:17], None, sub).then_inc(mixs_dve, 1)
            dve.wait_ge(mixs_exp, 1)
            dve.tensor_reduce(lg[:, 17:18], lg[:, 8:8 + MIX], AX.X, add).then_inc(mixs_dve, 1)
            dve.wait_ge(mixs_dve, 4)
            dve.reciprocal(lg[:, 18:19], lg[:, 17:18]).then_inc(mixs_dve, 1)
            dve.wait_ge(mixs_dve, 5)
            dve.tensor_scalar(lg[:, 0:MIX], lg[:, 8:8 + MIX], lg[:, 18:19], None, mult).then_inc(mixs_dve, 1)
            dve.wait_ge(mixs_dve, 6)
            dve.tensor_tensor(diag_att[0:B, :].rearrange("p (q k) -> p q k", k=MIX),
                              lg[:, 0:MIX].unsqueeze(1).to_broadcast((B, NB4, MIX)),
                              st("qmask")[0:B, :].unsqueeze(2).to_broadcast((B, NB4, MIX)), mult)\
               .then_inc(mixs_dve, 1)
            dve.wait_ge(mlp_mm, 4)
            dve.tensor_copy(mix_att[:], small[:, 0:NB4 * MIX].rearrange("p (q k) -> p q k", k=MIX))\
               .then_inc(mixs_dve, 1)
            dve.wait_ge(mixs_dve, 8)

            def mix_reduce(g, first):
                dve.wait_ge(mix_prod, g + 1)
                dve.tensor_reduce(mix_a[:].rearrange("p q o -> p (q o)"),
                                  soft[:, 1, :].rearrange("p (n k) -> p n k", k=MIX), AX.X, add)\
                   .then_inc(mix_red, 1)
                dve.wait_ge(mix_red, g + 1)
                if not first:
                    dve.wait_ge(c1_mm, 2 * g)
                dve.tensor_copy(mix_hl[:, HI], mix_a[:]).then_inc(mix_split, 1)
                dve.wait_ge(mix_split, 2 * g + 1)
                dve.tensor_tensor(mix_hl[:, LO], mix_a[:], mix_hl[:, HI].bitcast(F32), sub).then_inc(mix_split, 1)

            dve.wait_ge(bank_kept, 1)
            dve.wait_ge(ctx_mm, 4)
            for q in range(NQ):
                last = dve.tensor_tensor(
                    soft[:, 1, q * 256:(q + 1) * 256].rearrange("p (o k) -> p o k", k=MIX),
                    mix_att[:, q:q + 1, :].to_broadcast((P, SEQ, MIX)),
                    keep_bank[:].rearrange("p (o k) -> p o k", k=MIX), mult)
            last.then_inc(mix_prod, 1)
            dve.tensor_tensor(diag_att.rearrange("p (q k) -> p q k", k=MIX), mix_att[:],
                              st("kdiag").unsqueeze(1).to_broadcast((P, NB4, MIX)), mult).then_inc(mixs_dve, 1)
            mix_reduce(0, True)
            dve.wait_ge(mixs_dve, 9)
            dve.tensor_reduce(attd[:], diag_att.rearrange("p (q k) -> p q k", k=MIX), AX.X, add)\
               .then_inc(mixs_dve, 1)
            ctx_add_bias(2)
            ctx_add_bias(3)
            split_weight(2)
            split_weight(3)

            def c1_bias(g, first):
                for k in range(2):
                    if first:
                        dve.wait_ge(agg_done, 1)
                    dve.wait_ge(c1_mm, 2 * g + k + 1)
                    dve.tensor_tensor(tmp[:, k, :].rearrange("p (t n) -> p t n", t=2),
                                      feat[k][:].rearrange("p (t n) -> p t n", t=2),
                                      aggb[:, bass.ds(g * GT, GT)].unsqueeze(1).to_broadcast((P, 2, GT)), add)\
                       .then_inc(c1_t, 1)

            def kv(g):
                dve.wait_ge(kv_mm, g + 1)
                dve.tensor_scalar(kvt, small[:, 0:GT], kp("kvscale"), None, mult).then_inc(kv_t, 1)
                dve.wait_ge(kv_hi, g + 1)
                dve.tensor_tensor(kv_hl[:, LO, :], kvt, kv_hl[:, HI, :].bitcast(F32), sub).then_inc(kv_lo, 1)
                dve.wait_ge(kv_lo, g + 1)
                dve.transpose(vnat, kv_hl.bitcast(F32).rearrange("p s n -> p (s n)")).then_inc(v_tr, 1)

            def q_rest(g):
                for k in range(2):
                    dve.wait_ge(q_hi, 2 * g + k + 1)
                    dve.tensor_tensor(q_half(LO, k), feat[k][:].rearrange("p (c b s) -> p b c s", c=2, b=GB),
                                      q_half(HI, k).bitcast(F32), sub).then_inc(q_lo, 1)

            def s_biased(g, p, first):
                n = PAIRS * g + p
                dve.wait_ge(s_mm, n + 1)
                if p == 3:
                    dve.wait_ge(s_tr, n - 2)
                elif not first:
                    dve.wait_ge(s_tr, PAIRS * g)
                s = soft[:, p % 3, :]
                dve.tensor_tensor(s.rearrange("p (b n) -> p b n", b=2), sc[p % 2][:].rearrange("p (b n) -> p b n", b=2),
                                  kp("alibi").unsqueeze(1).to_broadcast((P, 2, GT)), add).then_inc(s_bias, 1)
                dve.wait_ge(s_bias, n + 1)
                dve.tensor_reduce(smx[:, p, :], heads(s), AX.X, ALU.max).then_inc(s_max, 1)

            def s_total(g, p):
                n = PAIRS * g + p
                dve.wait_ge(s_exp, n + 1)
                dve.tensor_reduce(ssum[:, p, :], heads(soft[:, p % 3, :]), AX.X, add).then_inc(s_sum, 1)
                dve.wait_ge(s_sum, n + 1)
                dve.reciprocal(srec[:, p, :], ssum[:, p, :]).then_inc(s_rec, 1)

            def s_transpose(g, p, first):
                n = PAIRS * g + p
                dve.wait_ge(s_norm, n + 1)
                if not first or p >= 2:
                    dve.wait_ge(p_lo, n - 1)
                dve.transpose(soft[:, 3 + p % 2, :], soft[:, p % 3, :]).then_inc(s_tr, 1)

            def probs_rest(g, p):
                dve.wait_ge(p_hi, PAIRS * g + p + 1)
                sl = [probsT[:, s, 2 * p:2 * p + 2].rearrange("p a b c -> p (a b c)") for s in (HI, LO)]
                dve.tensor_tensor(sl[LO], soft[:, 3 + p % 2, :], sl[HI].bitcast(F32), sub).then_inc(p_lo, 1)

            def o_rest(b):
                for q in range(NQ):
                    dve.wait_ge(o_hi, NQ * b + q + 1)
                    sl = [o_h[:, s, :, q * P:(q + 1) * P].rearrange("p h (b s) -> p b h s", b=4) for s in (HI, LO)]
                    dve.tensor_tensor(sl[LO], sc[q][:].rearrange("p (b h s) -> p b h s", b=4, h=4),
                                      sl[HI].bitcast(F32), sub).then_inc(o_lo, 1)

            def attn_residual(b):
                for q in range(NQ):
                    dve.wait_ge(x1_in[q], 16 * (b + 1))
                    dve.wait_ge(wo_mm, NQ * b + q + 1)
                    dve.tensor_tensor(x1[:, q, :], row[q][:], x1[:, q, :], add).then_inc(x1_add, 1)

            def y_context(b, with_front):
                for q in range(NQ):
                    dve.wait_ge(y_mm, NQ * b + q + 1)
                    if with_front:
                        dve.wait_ge(c1_lo, 2 * (b + 2))
                        dve.wait_ge(v_ready, b + 2)
                    yt = tmp[:, q, :].rearrange("p (t b o) -> p b t o", t=PH, b=4)
                    dve.tensor_tensor(
                        yt, ybank[q][:].rearrange("p (b t o) -> p b t o", t=PH, b=4),
                        ctxb[:, bass.ds(b * GT + q * P, P)].rearrange("p (b o) -> p b o", b=4).unsqueeze(2)
                        .to_broadcast((P, 4, PH, SEQ)), add).then_inc(y_t, 1)
                    dve.wait_ge(y_t, NQ * b + q + 1)
                    dve.tensor_reduce(ysum[:, :, 4 * q:4 * q + 4],
                                      tmp[:, q, :].rearrange("p (t b o) -> p t b o", t=PH, b=4), AX.X, add)\
                       .then_inc(y_sum, 1)

            def coef_1(b):
                dve.wait_ge(co_mm, 2 * b + 1)
                dve.tensor_copy(co[:, 0, 0:GB], small[:, 0:GB]).then_inc(co_dve, 1)
                dve.wait_ge(co_dve, CO * b + 1)
                dve.tensor_tensor(co[:, 1, :].rearrange("p (b e) -> p b e", e=EXPERTS),
                                  co[:, 0, 0:GB].unsqueeze(2).to_broadcast((P, GB, EXPERTS)),
                                  kp("keysT").unsqueeze(1).to_broadcast((P, GB, EXPERTS)), mult)\
                   .then_inc(co_dve, 1)

            def coef_2(b):
                lg = small[:, 64:64 + GB * EXPERTS].rearrange("p (b e) -> p b e", e=EXPERTS)
                ex = co[:, 3, :].rearrange("p (b e) -> p b e", e=EXPERTS)
                dve.wait_ge(co_mm, 2 * b + 2)
                dve.tensor_reduce(comx[:, 0, :], lg, AX.X, ALU.max).then_inc(co_dve, 1)
                dve.wait_ge(co_dve, CO * b + 3)
                dve.tensor_tensor(co[:, 2, :].rearrange("p (b e) -> p b e", e=EXPERTS), lg,
                                  comx[:, 0, :].unsqueeze(2).to_broadcast((P, GB, EXPERTS)), sub)\
                   .then_inc(co_dve, 1)
                return ex

            def coef_3(b):
                ex = co[:, 3, :].rearrange("p (b e) -> p b e", e=EXPERTS)
                dve.wait_ge(co_exp, b + 1)
                dve.tensor_reduce(comx[:, 1, :], ex, AX.X, add).then_inc(co_dve, 1)
                dve.wait_ge(co_dve, CO * b + 5)
                dve.reciprocal(comx[:, 2, :], comx[:, 1, :]).then_inc(co_dve, 1)
                dve.wait_ge(co_dve, CO * b + 6)
                dve.tensor_tensor(ex, ex, comx[:, 2, :].unsqueeze(2).to_broadcast((P, GB, EXPERTS)), mult)\
                   .then_inc(co_dve, 1)
                dve.wait_ge(co_dve, CO * b + 7)
                pairs = co[:, 3, :].rearrange("p (b c e) -> p c b e", c=EXPERTS // 2, e=2)
                dve.tensor_scalar(coef[:, 0], pairs[:, :, :, 0], kp("even"), None, mult).then_inc(co_dve, 1)
                dve.wait_ge(co_dve, CO * b + 8)
                dve.scalar_tensor_tensor(out=coef[:, 1], in0=pairs[:, :, :, 1], scalar=kp("odd"),
                                         in1=coef[:, 0], op0=mult, op1=add).then_inc(co_dve, 1)

            def hidden(b):
                for k in range(2):
                    dve.wait_ge(h_mm, 2 * b + k + 1)
                    dve.wait_ge(co_dve, CO * (b + 1))
                    dve.wait_ge(y_lo, NQ * b + k + 1)
                    dve.wait_ge(y_sum, NQ * b + k + 1)
                    dve.tensor_tensor(
                        tmp[:, k, :].rearrange("p (e b s) -> p e b s", e=2, b=GB),
                        feat[k][:].rearrange("p (e b s) -> p e b s", e=2, b=GB),
                        coef[:, 1, 2 * k:2 * k + 2, :].unsqueeze(3).to_broadcast((P, 2, GB, SEQ)), mult)\
                       .then_inc(h_t, 1)

            def out_residual(b):
                for q in range(NQ):
                    dve.wait_ge(out_mm, NQ * b + q + 1)
                    dve.wait_ge(xph_in[q], 16 * 4 * PH * (b + 1))
                    dve.tensor_tensor(x1[:, q, :], row[q][:], x1[:, q, :], add).then_inc(out_add, 1)

            c1_bias(0, True)
            kv(0)
            q_rest(0)
            s_biased(0, 0, True)
            s_biased(0, 1, True)
            s_total(0, 0)
            s_biased(0, 2, True)
            s_total(0, 1)
            s_transpose(0, 0, True)
            s_biased(0, 3, True)
            s_total(0, 2)
            s_transpose(0, 1, True)
            probs_rest(0, 0)
            s_total(0, 3)
            s_transpose(0, 2, True)
            probs_rest(0, 1)
            s_transpose(0, 3, True)
            probs_rest(0, 2)
            probs_rest(0, 3)
            mix_reduce(1, False)

            def body(g, last):
                o_rest(g - 1)
                c1_bias(g, False)
                attn_residual(g - 1)
                kv(g)
                q_rest(g)
                y_context(g - 1, True)
                s_biased(g, 0, False)
                s_biased(g, 1, False)
                coef_1(g - 1)
                s_total(g, 0)
                s_total(g, 1)
                coef_2(g - 1)
                s_biased(g, 2, False)
                s_transpose(g, 0, False)
                coef_3(g - 1)
                hidden(g - 1)
                s_biased(g, 3, False)
                s_transpose(g, 1, False)
                s_total(g, 2)
                probs_rest(g, 0)
                probs_rest(g, 1)
                s_total(g, 3)
                s_transpose(g, 2, False)
                s_transpose(g, 3, False)
                probs_rest(g, 2)
                probs_rest(g, 3)
                if not last:
                    mix_reduce(g + 1, False)
                out_residual(g - 1)

            with dve.Fori(1, GROUPS - 1) as g:
                body(g, False)
            body(GROUPS - 1, True)
            b = GROUPS - 1
            o_rest(b)
            attn_residual(b)
            y_context(b, False)
            coef_1(b)
            coef_2(b)
            coef_3(b)
            hidden(b)
            out_residual(b)


def kernel(**inputs):
    import numpy as np
    import concourse.bacc as bacc
    from concourse.bass_utils import run_bass_kernel_spmd

    a = {k: np.asarray(v) for k, v in inputs.items()}
    f32 = np.float32
    J = DIM // PH

    def by_phase(rows):
        return rows.reshape(J, PH, -1)

    def cols_by_phase(m):
        return m.reshape(m.shape[0], J, PH).transpose(0, 2, 1).reshape(m.shape[0], DIM)

    def spread_rows(m, n=P):
        return np.broadcast_to(m.reshape(1, -1), (n, m.size))

    x = np.ascontiguousarray(cols_by_phase(a["x"].reshape(TOK, DIM)))

    wo = a["L0_attn_Wo"].reshape(4, 2, 4, HD, DIM).transpose(1, 0, 3, 2, 4)
    down = a["L0_ffn_lora_down"].transpose(1, 0, 2).reshape(DIM, EXPERTS * RANK)
    up = a["L0_ffn_lora_up"].reshape(PH, P, DIM).transpose(1, 0, 2)
    weights = {
        "wq": by_phase(a["L0_attn_Wq"]),
        "wo": cols_by_phase(np.ascontiguousarray(wo).reshape(-1, DIM)),
        "wd": by_phase(down),
        "worg": by_phase(cols_by_phase(np.ascontiguousarray(a["L0_ffn_W_org"].T))),
        "wu": cols_by_phase(np.ascontiguousarray(up).reshape(-1, DIM)),
    }
    weights = {k: np.ascontiguousarray(v.reshape(P, PH * DIM)) for k, v in weights.items()}

    conv_w = a["L0_cond2_weight"]
    width, taps = conv_w.shape[1], conv_w.shape[2]
    wconv = np.zeros((PH, SEQ, 3, PH, SEQ), f32)
    for r in range(PH):
        for tap in range(taps):
            m = r + tap - taps // 2
            for o in range(SEQ):
                i0 = o // width * width
                wconv[m % PH, i0:i0 + width, m // PH + 1, r, o] = conv_w[o, :, tap]
    kvc = np.concatenate([by_phase(a["L0_attn_Wkv"]).reshape(P, -1), wconv.reshape(P, -1)], axis=1)

    p = np.arange(P)
    first = 2.0 ** (-2.0 ** (-(np.log2(HEADS) - 3)))
    slopes = np.array([first ** (i + 1) for i in range(HEADS)], dtype=f32)
    pos = np.arange(SEQ)
    far = (pos[None, :] - pos[:, None]).astype(f32)
    alibi = slopes.reshape(4, 1, HC, 1) * far[None, :, None, :]
    alibi = np.where((far <= 0)[None, :, None, :], alibi, f32(-1e30)).astype(f32).reshape(P, HC * SEQ)
    kernels = a["L0_cond_weight"][..., 0]
    bank_bias = np.zeros((4, SEQ, 4, SEQ), f32)
    for b in range(4):
        bank_bias[b, 0:MIX, b, :] = a["L0_cond_bias_k"]

    sel = np.zeros((P, P), f32)
    sel[0:BATCH] = np.arange(BATCH)[:, None] % 4 == p[None, :] // SEQ
    qmask = np.zeros((P, BATCH // 4), f32)
    qmask[0:BATCH] = np.arange(BATCH)[:, None] // 4 == np.arange(BATCH // 4)[None, :]

    start = dict(
        sel=sel, qmask=qmask, condT=a["cond_128"].T, w0=a["L0_cond_W0"], w1=a["L0_cond_W1"], w2=a["L0_cond_W2"],
        b0=a["L0_cond_b0"].reshape(P, 1), b1=a["L0_cond_b1"].reshape(P, 1), b2=spread_rows(a["L0_cond_b2"]),
        bank_bias=bank_bias.reshape(P, P),
        bank_w=np.tile(kernels.transpose(2, 1, 0).reshape(SEQ, SEQ * MIX), (4, 1)),
        kdiag=(p[:, None] % SEQ == np.arange(MIX)[None, :]).astype(f32),
        cwT=a["L0_cond2_c_weight"].T, fside=spread_rows(a["fside_S_0"]))
    keep = dict(
        alibi=alibi, kvscale=np.where(p % 32 < HD, HD ** -0.5, 1.0).astype(f32).reshape(P, 1),
        quad=(p[:, None] // 32 == np.arange(4)[None, :]).astype(f32),
        even=(p < RANK).astype(f32).reshape(P, 1), odd=(p >= RANK).astype(f32).reshape(P, 1),
        keysT=a["L0_ffn_lora_keys"].T,
        wq2=by_phase(np.ascontiguousarray(a["L0_ffn_Wq"].T)).reshape(P, -1), ones=np.ones((P, P), f32))
    arrays = {
        "x": x,
        "start": np.concatenate([start[n] for n in START], axis=1),
        "keep": np.concatenate([keep[n] for n in KEEP], axis=1),
        "kvc": kvc, **weights,
    }
    arrays = {f"in_{k}": np.ascontiguousarray(v) for k, v in arrays.items()}

    nc = bacc.Bacc("TRN2", target_bir_lowering=False, num_devices=1)
    d = {k: nc.dram_tensor(k, v.shape, F32, kind="ExternalInput").ap() for k, v in arrays.items()}
    out = nc.dram_tensor("out", (TOK, DIM), F32, kind="ExternalOutput").ap()
    build(nc, d["in_x"], d["in_start"], d["in_keep"], d["in_kvc"], {n: d[f"in_{n}"] for n in WEIGHTS}, out)
    r = run_bass_kernel_spmd(nc, [arrays], core_ids=[0])
    got = r.results[0]["out"]
    return got.reshape(BATCH, SEQ, PH, J).transpose(0, 1, 3, 2).reshape(BATCH, SEQ, DIM)
```

```python
import concourse.bass as bass
from concourse import mybir
from contextlib import ExitStack

F32 = mybir.dt.float32
F32R = mybir.dt.float32r
ALU = mybir.AluOpType
ACT = mybir.ActivationFunctionType
AX = mybir.AxisListType

P = 128
BATCH, SEQ, DIM = 64, 32, 512
TOK = BATCH * SEQ
GROUPS = 8
GT = TOK // GROUPS
GB = GT // SEQ
NQ = GT // P
PH = DIM // P
HEADS, HD = 32, 16
HC = P // HD
PAIRS = GB // 2
EXPERTS, RANK = 8, 64
MIX = 8
HI, LO = 0, 1

START = dict(sel=128, qmask=16, condT=64, w0=128, w1=128, w2=8, b0=1, b1=1, b2=8, bank_bias=128, bank_w=256, kdiag=8,
             cwT=128, fside=1)
KEEP = dict(alibi=256, kvscale=1, quad=4, lane=4, even=1, odd=1, keysT=8, wq2=512, ones=128, ident=128)


def columns(pack):
    at, out = 0, {}
    for name, n in pack.items():
        out[name] = (at, at + n)
        at += n
    return out, at


START_AT, START_N = columns(START)
KEEP_AT, KEEP_N = columns(KEEP)
WEIGHTS = ["wq", "wo", "wd", "worg", "wu"]


def build(nc, x_d, start_d, keep_d, kvc_d, w_d, swap_d, out_d):
    ctx = ExitStack()
    with ctx:
        def sb(name, shape, dt=F32):
            return ctx.enter_context(nc.sbuf_tensor(name, shape, dt))

        def sem(name):
            return ctx.enter_context(nc.semaphore(name))

        W = {n: sb(n, [P, 2, PH, DIM], F32R) for n in WEIGHTS}
        wkv = sb("wkv", [P, 2, PH, 4, 2 * HD], F32R)
        wconv = sb("wconv", [P, 2, 3, P], F32R)
        keep = sb("keep", [P, KEEP_N])
        c1_y = sb("c1_y", [P, 2, PH, GT], F32R)
        o_h = sb("o_h", [P, 2, PH, GT], F32R)
        q_x = sb("q_x", [P, 2, PH * GT], F32R)
        kdiag = sb("kdiag", [P, 2, HC, GT], F32R)
        vdiag = sb("vdiag", [P, 2, GB, 2, 4, HD], F32R)
        probsT = sb("probsT", [P, 2, GB, HC, SEQ], F32R)
        xphase = sb("xphase", [P, 2, GB, P + 2], F32R)
        xin = sb("xin", [P, NQ * DIM])
        x1 = sb("x1", [P, NQ, DIM])
        tmp = sb("tmp", [P, 2, DIM])
        soft = sb("soft", [P, 5, DIM])
        aggb = sb("aggb", [P, TOK])
        ctxb = sb("ctxb", [P, BATCH])
        mixd = sb("mixd", [P, 2, NQ, 4, SEQ], F32R)
        mix_att = sb("mix_att", [P, BATCH // 4, MIX])
        mix_a = sb("mix_a", [P, NQ, SEQ])
        mix_hl = sb("mix_hl", [P, 2, NQ, SEQ], F32R)
        smx = sb("smx", [P, PAIRS, 2 * HC])
        ssum = sb("ssum", [P, PAIRS, 2 * HC])
        srec = sb("srec", [P, PAIRS, 2 * HC])
        ysum = sb("ysum", [P, PH, GB])
        co = sb("co", [P, 4, GB * EXPERTS])
        comx = sb("comx", [P, 3, GB])
        coef = sb("coef", [P, 2, EXPERTS // 2, GB])
        attd = sb("attd", [P, BATCH // 4])
        mixs = sb("mixs", [P, 24])
        keep_bank = sb("keep_bank", [P, SEQ * MIX])
        hmlp = aggb[:, 0:2 * BATCH].rearrange("p (a b) -> p a b", a=2)
        diag_att = aggb[:, DIM:DIM + BATCH // 4 * MIX]
        start = soft[:, 3:5, :].rearrange("p a b -> p (a b)")

        def st(name):
            a, b = START_AT[name]
            return start[:, a:b]

        def kp(name):
            a, b = KEEP_AT[name]
            return keep[:, a:b]

        def q_half(s, k):
            return q_x[:, s, :].rearrange("p (b c s) -> p b c s", b=GB, c=PH)[:, :, 2 * k:2 * k + 2, :]

        def av_part(half, q):
            return avbank[q][0:64].rearrange("p a (b h s) -> p (a b) h s", b=2, h=HC)[:, :, 4 * half:4 * half + 4]

        def o_part(s, half, q):
            return o_h[64 * half:64 * half + 64, s, :, q * P:(q + 1) * P].rearrange("p h (s b) -> p b h s", b=4)

        def yt_view(q):
            return ytbank[q].rearrange("p (b t o) -> p b t o", b=4, t=PH)

        def y_part(s, q):
            return c1_y[:, s, :, q * P:(q + 1) * P].rearrange("p t (o b) -> p b t o", b=4)

        ones = kp("ones")
        kvt = tmp[:, 0, 0:GT]
        kv_hl = soft[:, 3, :].bitcast(F32R).rearrange("p (s n) -> p s n", s=2)
        vnat = tmp[:, 1, :]
        kv_in = tmp[:, 0, 0:128].rearrange("p (t n) -> p t n", t=PH)

        def pb(name, banks=1):
            return ctx.enter_context(nc.psum_tensor(name, [P, banks, DIM], F32))

        feat, score, aux = pb("feat", 2), pb("score", 2), pb("aux", 2)
        rows = [pb(f"rows{q}") for q in range(NQ)]
        feat, sc = [feat[:, k, :] for k in range(2)], [score[:, k, :] for k in range(2)]
        row = [r[:, 0, :] for r in rows]
        small = aux[:, 1, :]
        ybank = [aux[:, 0, :], feat[0]]
        ytbank = [feat[1], aux[:, 0, :]]
        avbank = [score, aux]

        start_in, keep_in, kvc_in = sem("start_in"), sem("keep_in"), sem("kvc_in")
        stage_in = [sem(f"stage_in{u}") for u in range(3)]
        x_in, x1_in = sem("x_in"), [sem(f"x1_in{q}") for q in range(NQ)]
        k_spread = sem("k_spread")
        xph_in = [sem(f"xph_in{q}") for q in range(NQ)]
        out_done = [sem(f"out_done{q}") for q in range(NQ)]
        zeroed = sem("zeroed")
        w_hi, w_lo, kvc_hi, kvc_lo = sem("w_hi"), sem("w_lo"), sem("kvc_hi"), sem("kvc_lo")
        mlp_mm, mlp_act, mixs_dve, mixs_exp, bank_kept = (sem("mlp_mm"), sem("mlp_act"), sem("mixs_dve"),
                                                          sem("mixs_exp"), sem("bank_kept"))
        ctx_mm, ctx_done = sem("ctx_mm"), sem("ctx_done")
        agg_outer, agg_mm, agg_done = sem("agg_outer"), sem("agg_mm"), sem("agg_done")
        mix_prod, mix_red, mix_split, mix_ready = (sem("mix_prod"), sem("mix_red"), sem("mix_split"),
                                                   sem("mix_ready"))
        x_hi, x_lo = sem("x_hi"), sem("x_lo")
        c1_mm, c1_t, c1_hi, c1_lo = sem("c1_mm"), sem("c1_t"), sem("c1_hi"), sem("c1_lo")
        kv_mm, kv_t, kv_hi, kv_lo, v_tr, v_ready = (sem("kv_mm"), sem("kv_t"), sem("kv_hi"), sem("kv_lo"),
                                                    sem("v_tr"), sem("v_ready"))
        q_mm, q_hi, q_lo = sem("q_mm"), sem("q_hi"), sem("q_lo")
        s_mm, s_bias, s_max, s_sub, s_exp, s_sum, s_rec, s_norm, s_tr, p_hi, p_lo = (
            sem("s_mm"), sem("s_bias"), sem("s_max"), sem("s_sub"), sem("s_exp"), sem("s_sum"),
            sem("s_rec"), sem("s_norm"), sem("s_tr"), sem("p_hi"), sem("p_lo"))
        av_mm, o_hi, o_lo = sem("av_mm"), sem("o_hi"), sem("o_lo")
        wo_mm, x1_add = sem("wo_mm"), sem("x1_add")
        xph_hi, xph_lo = sem("xph_hi"), sem("xph_lo")
        y_mm, y_t, yt_mm, y_sum, y_hi, y_lo = sem("y_mm"), sem("y_t"), sem("yt_mm"), sem("y_sum"), sem("y_hi"), sem("y_lo")
        co_mm, co_dve, co_exp = sem("co_mm"), sem("co_dve"), sem("co_exp")
        h_mm, h_t, h_hi, h_lo = sem("h_mm"), sem("h_t"), sem("h_hi"), sem("h_lo")
        out_mm, out_add = sem("out_mm"), sem("out_add")

        swap_out = [sem(f"swap_out{q}") for q in range(NQ)]
        swap_rows = [swap_d[q].rearrange("t i m j -> (i m) t j") for q in range(NQ)]
        swap_cols = [swap_d[q].rearrange("t i m j -> (t i) (m j)") for q in range(NQ)]

        x_g = x_d.rearrange("(g q p) c -> p g q c", q=NQ, p=P)
        out_g = out_d.rearrange("(g q p) c -> p g q c", q=NQ, p=P)

        NW = len(WEIGHTS) * PH
        EARLY = 12

        def slot_of(n):
            return n % 3 if n < EARLY else n % 2

        def stage(n):
            u = slot_of(n)
            return soft[:, 2, :] if u == 2 else x1[:, u, :]

        def stage_count(n):
            return sum(1 for m in range(n + 1) if slot_of(m) == slot_of(n))

        NB4 = BATCH // 4
        CO = 9

        block = ctx.enter_context(nc.Block())

        @block.sync
        def _(sp):
            sp.dma_start(start[:, 0:START_N], start_d).then_inc(start_in, 16)
            sp.dma_start(xin[:].rearrange("p (q c) -> p q c", q=NQ), x_g[:, 0]).then_inc(x_in, 16)
            sp.dma_start(keep[:], keep_d).then_inc(keep_in, 16)
            sp.dma_start(tmp[:, 0, :], kvc_d).then_inc(kvc_in, 16)

            def load_weight(n):
                prev = [m for m in range(n) if slot_of(m) == slot_of(n)]
                if prev:
                    sp.wait_ge(w_hi, prev[-1] + 1)
                    sp.wait_ge(w_lo, prev[-1] + 1)
                name, c = WEIGHTS[n // PH], n % PH
                sp.dma_start(stage(n), w_d[name][:, c * DIM:(c + 1) * DIM]).then_inc(stage_in[slot_of(n)], 16)

            def spread_k(g):
                if type(g) is int and g == 0:
                    sp.wait_ge(zeroed, 3)
                sp.wait_ge(kv_hi, g + 1)
                sp.wait_ge(kv_lo, g + 1)
                for h in range(HC):
                    src = 32 * (h % 4)
                    sp.dma_start(kdiag[HD * h:HD * (h + 1), :, h, :].bitcast(F32),
                                 kv_hl[src:src + HD, :, :].bitcast(F32)).then_inc(k_spread, 16)

            def load_x(g):
                sp.dma_start(xin[:].rearrange("p (q c) -> p q c", q=NQ),
                             x_g[:, bass.ds(g, 1)].squeeze(1)).then_inc(x_in, 16)

            def load_x1(g, q):
                sp.dma_start(x1[:, q, :], x_g[:, bass.ds(g, 1), q].squeeze(1)).then_inc(x1_in[q], 16)

            def by_phase(b):
                for q in range(NQ):
                    sp.wait_ge(x1_add, NQ * b + q + 1)
                    sp.dma_start(swap_rows[q], x1[:, q, :].rearrange("p (t j) -> p t j", t=PH)).then_inc(swap_out[q], 16)
                for q in range(NQ):
                    sp.wait_ge(swap_out[q], 16 * (b + 1))
                    sp.dma_start(xin[:, q * DIM:(q + 1) * DIM], swap_cols[q]).then_inc(xph_in[q], 16)

            def store(b, last):
                for q in range(NQ):
                    sp.wait_ge(out_add, NQ * b + q + 1)
                    sp.dma_start(out_g[:, bass.ds(b, 1), q].squeeze(1), x1[:, q, :]).then_inc(out_done[q], 16)
                for q in range(NQ):
                    sp.wait_ge(out_done[q], 16 * (b + 1))
                    if not last:
                        load_x1(b + 1, q)

            for n in range(NW):
                load_weight(n)
                if n == 11:
                    spread_k(0)
                    sp.wait_ge(x_hi, 1)
                    sp.wait_ge(x_lo, NQ)
                    load_x(1)
            sp.wait_ge(w_hi, NW)
            sp.wait_ge(w_lo, NW)
            for q in range(NQ):
                load_x1(0, q)

            with sp.Fori(1, GROUPS - 1) as g:
                by_phase(g - 1)
                spread_k(g)
                sp.wait_ge(xph_hi, NQ * g)
                sp.wait_ge(xph_lo, NQ * g)
                load_x(g + 1)
                store(g - 1, False)
            by_phase(GROUPS - 2)
            spread_k(GROUPS - 1)
            store(GROUPS - 2, False)
            by_phase(GROUPS - 1)
            store(GROUPS - 1, True)

        @block.tensor
        def _(pe):
            def split_mm(out, a_hi, a_lo, b_hi, b_lo, first, last):
                pe.matmul(out, a_hi, b_hi, start=first, stop=False)
                pe.matmul(out, a_hi, b_lo, start=False, stop=False)
                return pe.matmul(out, a_lo, b_hi, start=False, stop=last)

            pe.wait_ge(zeroed, 3)

            pe.wait_ge(start_in, 16)
            pe.matmul(small[:, 0:BATCH], st("w0"), st("condT"), start=True, stop=True).then_inc(mlp_mm, 1)
            pe.matmul(sc[0][:, 0:BATCH], st("cwT"), st("condT"), start=True, stop=True).then_inc(ctx_mm, 1)
            pe.wait_ge(mlp_act, 1)
            pe.matmul(small[:, 0:BATCH], st("w1"), hmlp[:, 0, :], start=True, stop=True).then_inc(mlp_mm, 1)
            pe.wait_ge(mlp_act, 2)
            pe.matmul(small[0:BATCH, 0:MIX], hmlp[:, 1, :], st("w2"), start=True, stop=True).then_inc(mlp_mm, 1)

            pe.wait_ge(mixs_dve, 7)
            pe.matmul(small[:, 0:NB4 * MIX], st("sel")[0:BATCH, :], diag_att[0:BATCH, :],
                      start=True, stop=True).then_inc(mlp_mm, 1)

            def agg_part(c):
                pe.wait_ge(agg_outer, c + 1)
                if c == 0:
                    pe.wait_ge(keep_in, 16)
                    pe.wait_ge(ctx_done, 1)
                if c >= 2:
                    pe.wait_ge(agg_done, c - 1)
                pe.matmul(sc[c % 2], ones, soft[:, c % 2, :], start=True, stop=True).then_inc(agg_mm, 1)

            def mix(g):
                pe.wait_ge(x_hi, g + 1)
                pe.wait_ge(x_lo, NQ * (g + 1))
                pe.wait_ge(mix_ready, g + 1)
                for k in range(2):
                    for t in range(2 * k, 2 * k + 2):
                        for q in range(NQ):
                            at = (t % 2) * GT + q * P
                            xs = [q_x[:, s, q * DIM + t * P:q * DIM + (t + 1) * P] for s in (HI, LO)]
                            ms = [mixd[:, s, q].rearrange("p a b -> p (a b)") for s in (HI, LO)]
                            mm = split_mm(feat[k][:, at:at + P], xs[HI], xs[LO], ms[HI], ms[LO], True, True)
                    mm.then_inc(c1_mm, 1)

            def kv_and_q(g):
                pe.wait_ge(kvc_hi, 1)
                pe.wait_ge(kvc_lo, 1)
                for t in range(PH):
                    if t % 2 == 0:
                        pe.wait_ge(c1_hi, 2 * g + t // 2 + 1)
                        pe.wait_ge(c1_lo, 2 * g + t // 2 + 1)
                    ws = [wkv[:, s, t].rearrange("p r n -> p (r n)") for s in (HI, LO)]
                    mm = split_mm(small[:, 0:GT], ws[HI], ws[LO], c1_y[:, HI, t, :], c1_y[:, LO, t, :],
                                  t == 0, t == PH - 1)
                mm.then_inc(kv_mm, 1)
                pe.wait_ge(w_hi, PH)
                pe.wait_ge(w_lo, PH)
                for c in range(PH):
                    for t in range(PH):
                        ws = [W["wq"][:, s, t, c * P:(c + 1) * P] for s in (HI, LO)]
                        at = (c % 2) * GT
                        mm = split_mm(feat[c // 2][:, at:at + GT], ws[HI], ws[LO],
                                      c1_y[:, HI, t, :], c1_y[:, LO, t, :], t == 0, t == PH - 1)
                    if c % 2:
                        mm.then_inc(q_mm, 1)

            def scores(g, p):
                if p == 0:
                    pe.wait_ge(q_hi, 2 * (g + 1))
                    pe.wait_ge(q_lo, 2 * (g + 1))
                    pe.wait_ge(k_spread, 16 * HC * (g + 1))
                if p >= 2:
                    pe.wait_ge(s_bias, PAIRS * g + p - 1)
                for b in (2 * p, 2 * p + 1):
                    qs = [q_x[:, s, b * P:(b + 1) * P] for s in (HI, LO)]
                    ks = [kdiag[:, s, :, b * SEQ:(b + 1) * SEQ] for s in (HI, LO)]
                    at = (b % 2) * GT
                    mm = split_mm(sc[p % 2][:, at:at + GT], qs[HI], qs[LO], ks[HI], ks[LO], True, True)
                mm.then_inc(s_mm, 1)

            def attend(b):
                pe.wait_ge(v_ready, b + 1)
                for q in range(NQ):
                    pe.wait_ge(p_hi, PAIRS * b + 2 * q + 2)
                    pe.wait_ge(p_lo, PAIRS * b + 2 * q + 2)
                    for m in range(4):
                        n = 4 * q + m
                        vs = [vdiag[:, s, n].rearrange("p z c d -> p (z c d)") for s in (HI, LO)]
                        ps = [probsT[:, s, n].rearrange("p a b -> p (a b)") for s in (HI, LO)]
                        mm = split_mm(avbank[q][:, m // 2, m % 2 * GT:(m % 2 + 1) * GT],
                                      vs[HI], vs[LO], ps[HI], ps[LO], True, True)
                    mm.then_inc(av_mm, 1)

            def out_proj(b):
                pe.wait_ge(w_hi, 2 * PH)
                pe.wait_ge(w_lo, 2 * PH)
                for q in range(NQ):
                    pe.wait_ge(o_hi, 2 * (NQ * b + q + 1))
                    pe.wait_ge(o_lo, 2 * (NQ * b + q + 1))
                    for c in range(PH):
                        os = [o_h[:, s, c, q * P:(q + 1) * P] for s in (HI, LO)]
                        mm = split_mm(row[q], os[HI], os[LO], W["wo"][:, HI, c, :], W["wo"][:, LO, c, :],
                                      c == 0, c == PH - 1)
                    mm.then_inc(wo_mm, 1)

            def conv(b, with_front):
                for q in range(NQ):
                    pe.wait_ge(xph_hi, NQ * b + q + 1)
                    pe.wait_ge(xph_lo, NQ * b + q + 1)
                    if q == 1 and with_front:
                        pe.wait_ge(q_hi, 2 * (b + 1) + 1)
                        pe.wait_ge(q_lo, 2 * (b + 1) + 1)
                    for k in range(3):
                        xs = [xphase[:, s, 4 * q:4 * q + 4, k:k + P] for s in (HI, LO)]
                        mm = split_mm(ybank[q], wconv[:, HI, k, :], wconv[:, LO, k, :], xs[HI], xs[LO],
                                      k == 0, k == 2)
                    mm.then_inc(y_mm, 1)

            def transpose_y(b, with_front):
                for q in range(NQ):
                    pe.wait_ge(y_t, NQ * b + q + 1)
                    if q == 0 and with_front:
                        pe.wait_ge(q_lo, 2 * (b + 1) + 2)
                    for m in range(4):
                        mm = pe.transpose(ytbank[q][:, m * P:(m + 1) * P], tmp[:, q, m * P:(m + 1) * P], kp("ident"))
                    mm.then_inc(yt_mm, 1)

            def coef_query(b):
                pe.wait_ge(y_sum, NQ * (b + 1))
                for t in range(PH):
                    mm = pe.matmul(small[:, 0:GB], kp("wq2")[:, t * P:(t + 1) * P], ysum[:, t, :],
                                   start=(t == 0), stop=(t == PH - 1))
                mm.then_inc(co_mm, 1)

            def coef_scores(b):
                pe.wait_ge(co_dve, CO * b + 2)
                pe.matmul(small[:, 64:64 + GB * EXPERTS], ones, co[:, 1, :], start=True, stop=True)\
                  .then_inc(co_mm, 1)

            def lora_down(b, k):
                pe.wait_ge(w_hi, 3 * PH)
                pe.wait_ge(w_lo, 3 * PH)
                pe.wait_ge(y_hi, NQ * (b + 1))
                pe.wait_ge(y_lo, NQ * (b + 1))
                for e in (2 * k, 2 * k + 1):
                    for t in range(PH):
                        ws = [W["wd"][:, s, t, e * P:(e + 1) * P] for s in (HI, LO)]
                        at = (e % 2) * GT
                        mm = split_mm(feat[k][:, at:at + GT], ws[HI], ws[LO],
                                      c1_y[:, HI, t, :], c1_y[:, LO, t, :], t == 0, t == PH - 1)
                mm.then_inc(h_mm, 1)

            def base(q):
                if q == 0:
                    pe.wait_ge(w_hi, 4 * PH)
                    pe.wait_ge(w_lo, 4 * PH)
                for t in range(PH):
                    ys = [c1_y[:, s, t, q * P:(q + 1) * P] for s in (HI, LO)]
                    split_mm(row[q], ys[HI], ys[LO], W["worg"][:, HI, t, :], W["worg"][:, LO, t, :],
                             t == 0, False)

            def lora_up(b):
                pe.wait_ge(w_hi, 5 * PH)
                pe.wait_ge(w_lo, 5 * PH)
                pe.wait_ge(h_hi, 2 * (b + 1))
                pe.wait_ge(h_lo, 2 * (b + 1))
                for q in range(NQ):
                    for e in range(PH):
                        hs = [o_h[:, s, e, q * P:(q + 1) * P] for s in (HI, LO)]
                        mm = split_mm(row[q], hs[HI], hs[LO], W["wu"][:, HI, e, :], W["wu"][:, LO, e, :],
                                      False, e == PH - 1)
                    mm.then_inc(out_mm, 1)

            agg_part(0)
            mix(0)
            for c in range(1, 4):
                agg_part(c)
            kv_and_q(0)
            for p in range(PAIRS):
                if p == 0:
                    pe.wait_ge(agg_done, 4)
                scores(0, p)

            with pe.Fori(1, GROUPS) as g:
                attend(g - 1)
                mix(g)
                out_proj(g - 1)
                kv_and_q(g)
                conv(g - 1, True)
                scores(g, 0)
                scores(g, 1)
                transpose_y(g - 1, True)
                scores(g, 2)
                scores(g, 3)
                coef_query(g - 1)
                lora_down(g - 1, 0)
                coef_scores(g - 1)
                lora_down(g - 1, 1)
                base(0)
                base(1)
                lora_up(g - 1)
            b = GROUPS - 1
            attend(b)
            out_proj(b)
            conv(b, False)
            transpose_y(b, False)
            coef_query(b)
            lora_down(b, 0)
            coef_scores(b)
            lora_down(b, 1)
            base(0)
            base(1)
            lora_up(b)

        @block.scalar
        def _(act):
            def copy(out, in_):
                return act.activation(out, in_, ACT.Copy)

            act.wait_ge(mlp_mm, 1)
            act.activation(hmlp[:, 0, :], small[:, 0:BATCH], ACT.Gelu, bias=st("b0")).then_inc(mlp_act, 1)
            act.wait_ge(mlp_mm, 2)
            act.activation(hmlp[:, 1, :], small[:, 0:BATCH], ACT.Gelu, bias=st("b1")).then_inc(mlp_act, 1)

            def split_weight(n):
                act.wait_ge(stage_in[slot_of(n)], 16 * stage_count(n))
                copy(W[WEIGHTS[n // PH]][:, HI, n % PH, :], stage(n)).then_inc(w_hi, 1)

            def x_split(g):
                act.wait_ge(x_in, 16 * (g + 1))
                copy(q_x[:, HI, :], xin[:]).then_inc(x_hi, 1)

            def aggb_copy(c):
                act.wait_ge(agg_mm, c + 1)
                copy(aggb[:, c * DIM:(c + 1) * DIM], sc[c % 2]).then_inc(agg_done, 1)

            def c1_split(g):
                for k in range(2):
                    act.wait_ge(c1_t, 2 * g + k + 1)
                    copy(c1_y[:, HI, 2 * k:2 * k + 2, :].rearrange("p a b -> p (a b)"),
                         tmp[:, k, :]).then_inc(c1_hi, 1)

            def kvq_split(g):
                act.wait_ge(kv_t, g + 1)
                copy(kv_hl[:, HI, :], kvt).then_inc(kv_hi, 1)
                for k in range(2):
                    act.wait_ge(q_mm, 2 * g + k + 1)
                    copy(q_half(HI, k), feat[k].rearrange("p (c b s) -> p b c s", c=2, b=GB)).then_inc(q_hi, 1)

            def exp(g, p):
                act.wait_ge(s_sub, PAIRS * g + p + 1)
                act.activation(soft[:, p % 3, :], soft[:, p % 3, :], ACT.Exp).then_inc(s_exp, 1)

            def probs_split(g, p):
                act.wait_ge(s_tr, PAIRS * g + p + 1)
                copy(probsT[:, HI, 2 * p:2 * p + 2].rearrange("p a b c -> p (a b c)"),
                     soft[:, 3 + p % 2, :]).then_inc(p_hi, 1)

            def o_split(b):
                for q in range(NQ):
                    act.wait_ge(av_mm, NQ * b + q + 1)
                    for half in range(2):
                        copy(o_part(HI, half, q), av_part(half, q)).then_inc(o_hi, 1)

            def xph_split(b):
                for q in range(NQ):
                    act.wait_ge(xph_in[q], 16 * (b + 1))
                    copy(xphase[:, HI, 4 * q:4 * q + 4, 1:P + 1],
                         xin[:, q * DIM:(q + 1) * DIM].rearrange("p (b j) -> p b j", b=4)).then_inc(xph_hi, 1)

            def y_split(b):
                for q in range(NQ):
                    act.wait_ge(yt_mm, NQ * b + q + 1)
                    copy(y_part(HI, q), yt_view(q)).then_inc(y_hi, 1)

            def coef_exp(b):
                act.wait_ge(co_dve, CO * b + 4)
                act.activation(co[:, 3, :], co[:, 2, :], ACT.Exp,
                               scale=1.0 / (SEQ * 128.0 ** 0.5)).then_inc(co_exp, 1)

            def h_split(b):
                for k in range(2):
                    act.wait_ge(h_t, 2 * b + k + 1)
                    copy(o_h[:, HI, 2 * k:2 * k + 2, :].rearrange("p a b -> p (a b)"),
                         tmp[:, k, :]).then_inc(h_hi, 1)

            act.wait_ge(kvc_in, 16)
            copy(wkv[:, HI], kv_in.unsqueeze(2).to_broadcast((P, PH, 4, 2 * HD)))
            copy(wconv[:, HI].rearrange("p a b -> p (a b)"), tmp[:, 0, 128:512]).then_inc(kvc_hi, 1)
            x_split(0)
            for n in range(3):
                split_weight(n)
            act.wait_ge(mixs_dve, 3)
            act.activation(mixs[0:BATCH, 8:8 + MIX], mixs[0:BATCH, 0:MIX], ACT.Exp).then_inc(mixs_exp, 1)
            split_weight(3)
            aggb_copy(0)
            c1_split(0)
            for n in range(PH, 2 * PH):
                split_weight(n)
            for c in range(1, 4):
                aggb_copy(c)
            kvq_split(0)
            for n in range(2 * PH, EARLY):
                split_weight(n)
            exp(0, 0)
            exp(0, 1)
            exp(0, 2)
            probs_split(0, 0)
            exp(0, 3)
            probs_split(0, 1)
            probs_split(0, 2)
            probs_split(0, 3)
            for n in range(EARLY, NW):
                split_weight(n)
            act.wait_ge(s_mm, PAIRS)
            x_split(1)

            with act.Fori(1, GROUPS - 1) as g:
                o_split(g - 1)
                c1_split(g)
                kvq_split(g)
                xph_split(g - 1)
                exp(g, 0)
                y_split(g - 1)
                exp(g, 1)
                exp(g, 2)
                probs_split(g, 0)
                exp(g, 3)
                coef_exp(g - 1)
                probs_split(g, 1)
                h_split(g - 1)
                probs_split(g, 2)
                probs_split(g, 3)
                x_split(g + 1)
            g = GROUPS - 1
            o_split(g - 1)
            c1_split(g)
            kvq_split(g)
            xph_split(g - 1)
            exp(g, 0)
            y_split(g - 1)
            exp(g, 1)
            exp(g, 2)
            probs_split(g, 0)
            exp(g, 3)
            coef_exp(g - 1)
            probs_split(g, 1)
            h_split(g - 1)
            probs_split(g, 2)
            probs_split(g, 3)
            o_split(g)
            xph_split(g)
            y_split(g)
            coef_exp(g)
            h_split(g)

        @block.gpsimd
        def _(pool):
            def lo_of(out, whole, hi):
                return pool.tensor_tensor(out, whole, hi.bitcast(F32), ALU.subtract)

            pool.memset(kdiag[:].bitcast(F32).rearrange("p a b c -> p (a b c)"), 0.0).then_inc(zeroed, 1)
            pool.memset(vdiag[:].bitcast(F32).rearrange("p s b z c d -> p (s b z c d)"), 0.0).then_inc(zeroed, 1)
            pool.memset(xphase[:, :, :, 0:P + 2:P + 1].bitcast(F32), 0.0).then_inc(zeroed, 1)

            def split_weight(n):
                pool.wait_ge(w_hi, n + 1)
                pool.wait_ge(w_lo, n)
                w = W[WEIGHTS[n // PH]]
                lo_of(w[:, LO, n % PH, :], stage(n), w[:, HI, n % PH, :]).then_inc(w_lo, 1)

            def x_split(g):
                pool.wait_ge(x_hi, g + 1)
                for q in range(NQ):
                    sl = slice(q * DIM, (q + 1) * DIM)
                    lo_of(q_x[:, LO, sl], xin[:, sl], q_x[:, HI, sl]).then_inc(x_lo, 1)

            def mix_product(g):
                for q in range(NQ):
                    last = pool.tensor_tensor(
                        soft[:, 1, q * 256:(q + 1) * 256].rearrange("p (o k) -> p o k", k=MIX),
                        mix_att[:, bass.ds(NQ * g + q, 1), :].to_broadcast((P, SEQ, MIX)),
                        keep_bank[:].rearrange("p (o k) -> p o k", k=MIX), ALU.mult)
                return last

            def mix_diag(g):
                pool.wait_ge(mix_split, 2 * (g + 1))
                pool.tensor_tensor(
                    mixd[:].rearrange("p s q m o -> p (s q) m o"),
                    mix_hl[:].bitcast(F32).rearrange("p s q o -> p (s q) o").unsqueeze(2)
                    .to_broadcast((P, 2 * NQ, 4, SEQ)),
                    kp("lane").unsqueeze(1).unsqueeze(3).to_broadcast((P, 2 * NQ, 4, SEQ)),
                    ALU.mult).then_inc(mix_ready, 1)

            def c1_split(g):
                for k in range(2):
                    pool.wait_ge(c1_hi, 2 * g + k + 1)
                    sl = [c1_y[:, s, 2 * k:2 * k + 2, :].rearrange("p a b -> p (a b)") for s in (HI, LO)]
                    lo_of(sl[LO], tmp[:, k, :], sl[HI]).then_inc(c1_lo, 1)

            def v_spread(g):
                pool.wait_ge(zeroed, 3)
                pool.wait_ge(v_tr, g + 1)
                pool.tensor_tensor(
                    vdiag[:, :, :, 0].rearrange("p s b c d -> p (s b) c d"),
                    vnat.rearrange("p (n e) -> p n e", e=2 * HD)[:, :, HD:2 * HD].unsqueeze(2)
                    .to_broadcast((P, 2 * GB, 4, HD)),
                    kp("quad").unsqueeze(1).unsqueeze(3).to_broadcast((P, 2 * GB, 4, HD)),
                    ALU.mult).then_inc(v_ready, 1)

            def heads(ap):
                return ap.rearrange("p (h k) -> p h k", k=SEQ)

            def s_subtract(g, p):
                pool.wait_ge(s_max, PAIRS * g + p + 1)
                s = heads(soft[:, p % 3, :])
                pool.tensor_tensor(s, s, smx[:, p, :].unsqueeze(2).to_broadcast((P, 2 * HC, SEQ)),
                                   ALU.subtract).then_inc(s_sub, 1)

            def s_normalize(g, p):
                pool.wait_ge(s_rec, PAIRS * g + p + 1)
                s = heads(soft[:, p % 3, :])
                pool.tensor_tensor(s, s, srec[:, p, :].unsqueeze(2).to_broadcast((P, 2 * HC, SEQ)),
                                   ALU.mult).then_inc(s_norm, 1)

            def xph_split(b):
                for q in range(NQ):
                    pool.wait_ge(xph_hi, NQ * b + q + 1)
                    lo_of(xphase[:, LO, 4 * q:4 * q + 4, 1:P + 1],
                          xin[:, q * DIM:(q + 1) * DIM].rearrange("p (b j) -> p b j", b=4),
                          xphase[:, HI, 4 * q:4 * q + 4, 1:P + 1]).then_inc(xph_lo, 1)

            def h_split(b):
                for k in range(2):
                    pool.wait_ge(h_hi, 2 * b + k + 1)
                    sl = [o_h[:, s, 2 * k:2 * k + 2, :].rearrange("p a b -> p (a b)") for s in (HI, LO)]
                    lo_of(sl[LO], tmp[:, k, :], sl[HI]).then_inc(h_lo, 1)

            pool.wait_ge(kvc_hi, 1)
            lo_of(wkv[:, LO], kv_in.unsqueeze(2).to_broadcast((P, PH, 4, 2 * HD)), wkv[:, HI])
            lo_of(wconv[:, LO].rearrange("p a b -> p (a b)"), tmp[:, 0, 128:512],
                  wconv[:, HI].rearrange("p a b -> p (a b)")).then_inc(kvc_lo, 1)
            x_split(0)
            for c in range(4):
                pool.wait_ge(mixs_dve, 10)
                pool.wait_ge(mix_red, 1)
                if c >= 2:
                    pool.wait_ge(agg_mm, c - 1)
                pool.tensor_tensor(
                    soft[:, c % 2, :].rearrange("p (q n) -> p q n", q=4),
                    attd[:, 4 * c:4 * c + 4].unsqueeze(2).to_broadcast((P, 4, P)),
                    st("bank_bias").unsqueeze(1).to_broadcast((P, 4, P)), ALU.mult).then_inc(agg_outer, 1)
                if c == 0:
                    mix_diag(0)
            c1_split(0)
            for n in range(PH, 2 * PH):
                split_weight(n)
            v_spread(0)
            for n in range(2 * PH, EARLY):
                split_weight(n)
            s_subtract(0, 0)
            s_subtract(0, 1)
            s_normalize(0, 0)
            s_subtract(0, 2)
            s_normalize(0, 1)
            s_subtract(0, 3)
            s_normalize(0, 2)
            s_normalize(0, 3)
            pool.wait_ge(s_tr, 2)
            mix_product(1).then_inc(mix_prod, 1)
            for n in range(EARLY, NW):
                split_weight(n)
            x_split(1)
            mix_diag(1)

            def body(g, last):
                c1_split(g)
                v_spread(g)
                xph_split(g - 1)
                s_subtract(g, 0)
                s_subtract(g, 1)
                s_normalize(g, 0)
                s_subtract(g, 2)
                s_normalize(g, 1)
                s_subtract(g, 3)
                s_normalize(g, 2)
                h_split(g - 1)
                s_normalize(g, 3)
                if not last:
                    pool.wait_ge(s_tr, PAIRS * g + 2)
                    mix_product(g + 1).then_inc(mix_prod, 1)
                    x_split(g + 1)
                    mix_diag(g + 1)

            with pool.Fori(1, GROUPS - 1) as g:
                body(g, False)
            body(GROUPS - 1, True)
            b = GROUPS - 1
            xph_split(b)
            h_split(b)

        @block.vector
        def _(dve):
            add, sub, mult = ALU.add, ALU.subtract, ALU.mult

            def heads(ap):
                return ap.rearrange("p (h k) -> p h k", k=SEQ)

            def split_weight(n):
                dve.wait_ge(w_hi, n + 1)
                w = W[WEIGHTS[n // PH]]
                dve.tensor_tensor(w[:, LO, n % PH, :], stage(n), w[:, HI, n % PH, :].bitcast(F32), sub)\
                   .then_inc(w_lo, 1)

            dve.wait_ge(start_in, 16)
            dve.tensor_copy(keep_bank[:], st("bank_w")).then_inc(bank_kept, 1)
            dve.wait_ge(ctx_mm, 1)
            dve.tensor_scalar(ctxb[:], sc[0][:, 0:BATCH], st("fside"), None, add).then_inc(ctx_done, 1)
            split_weight(0)
            split_weight(1)
            lg, B = mixs[0:BATCH], BATCH
            dve.wait_ge(mlp_mm, 3)
            dve.tensor_tensor(lg[:, 0:MIX], small[0:B, 0:MIX], st("b2")[0:B, :], add).then_inc(mixs_dve, 1)
            dve.wait_ge(mixs_dve, 1)
            dve.tensor_reduce(lg[:, 16:17], lg[:, 0:MIX], AX.X, ALU.max).then_inc(mixs_dve, 1)
            dve.wait_ge(mixs_dve, 2)
            dve.tensor_scalar(lg[:, 0:MIX], lg[:, 0:MIX], lg[:, 16:17], None, sub).then_inc(mixs_dve, 1)
            dve.wait_ge(mixs_exp, 1)
            dve.tensor_reduce(lg[:, 17:18], lg[:, 8:8 + MIX], AX.X, add).then_inc(mixs_dve, 1)
            dve.wait_ge(mixs_dve, 4)
            dve.reciprocal(lg[:, 18:19], lg[:, 17:18]).then_inc(mixs_dve, 1)
            dve.wait_ge(mixs_dve, 5)
            dve.tensor_scalar(lg[:, 0:MIX], lg[:, 8:8 + MIX], lg[:, 18:19], None, mult).then_inc(mixs_dve, 1)
            dve.wait_ge(mixs_dve, 6)
            dve.tensor_tensor(diag_att[0:B, :].rearrange("p (q k) -> p q k", k=MIX),
                              lg[:, 0:MIX].unsqueeze(1).to_broadcast((B, NB4, MIX)),
                              st("qmask")[0:B, :].unsqueeze(2).to_broadcast((B, NB4, MIX)), mult)\
               .then_inc(mixs_dve, 1)
            dve.wait_ge(mlp_mm, 4)
            dve.tensor_copy(mix_att[:], small[:, 0:NB4 * MIX].rearrange("p (q k) -> p q k", k=MIX))\
               .then_inc(mixs_dve, 1)
            dve.wait_ge(mixs_dve, 8)

            def mix_reduce(g, first):
                dve.wait_ge(mix_prod, g + 1)
                dve.tensor_reduce(mix_a[:].rearrange("p q o -> p (q o)"),
                                  soft[:, 1, :].rearrange("p (n k) -> p n k", k=MIX), AX.X, add)\
                   .then_inc(mix_red, 1)
                dve.wait_ge(mix_red, g + 1)
                if not first:
                    dve.wait_ge(c1_mm, 2 * g)
                dve.tensor_copy(mix_hl[:, HI], mix_a[:]).then_inc(mix_split, 1)
                dve.wait_ge(mix_split, 2 * g + 1)
                dve.tensor_tensor(mix_hl[:, LO], mix_a[:], mix_hl[:, HI].bitcast(F32), sub).then_inc(mix_split, 1)

            dve.wait_ge(bank_kept, 1)
            for q in range(NQ):
                last = dve.tensor_tensor(
                    soft[:, 1, q * 256:(q + 1) * 256].rearrange("p (o k) -> p o k", k=MIX),
                    mix_att[:, q:q + 1, :].to_broadcast((P, SEQ, MIX)),
                    keep_bank[:].rearrange("p (o k) -> p o k", k=MIX), mult)
            last.then_inc(mix_prod, 1)
            dve.tensor_tensor(diag_att.rearrange("p (q k) -> p q k", k=MIX), mix_att[:],
                              st("kdiag").unsqueeze(1).to_broadcast((P, NB4, MIX)), mult).then_inc(mixs_dve, 1)
            mix_reduce(0, True)
            dve.wait_ge(mixs_dve, 9)
            dve.tensor_reduce(attd[:], diag_att.rearrange("p (q k) -> p q k", k=MIX), AX.X, add)\
               .then_inc(mixs_dve, 1)
            split_weight(2)
            split_weight(3)

            def c1_bias(g, first):
                for k in range(2):
                    if first:
                        dve.wait_ge(agg_done, 1)
                    dve.wait_ge(c1_mm, 2 * g + k + 1)
                    dve.tensor_tensor(tmp[:, k, :].rearrange("p (t n) -> p t n", t=2),
                                      feat[k].rearrange("p (t n) -> p t n", t=2),
                                      aggb[:, bass.ds(g * GT, GT)].unsqueeze(1).to_broadcast((P, 2, GT)), add)\
                       .then_inc(c1_t, 1)

            def kv(g):
                dve.wait_ge(kv_mm, g + 1)
                dve.tensor_scalar(kvt, small[:, 0:GT], kp("kvscale"), None, mult).then_inc(kv_t, 1)
                dve.wait_ge(kv_hi, g + 1)
                dve.tensor_tensor(kv_hl[:, LO, :], kvt, kv_hl[:, HI, :].bitcast(F32), sub).then_inc(kv_lo, 1)
                dve.wait_ge(kv_lo, g + 1)
                dve.transpose(vnat, kv_hl.bitcast(F32).rearrange("p s n -> p (s n)")).then_inc(v_tr, 1)

            def q_rest(g):
                for k in range(2):
                    dve.wait_ge(q_hi, 2 * g + k + 1)
                    dve.tensor_tensor(q_half(LO, k), feat[k].rearrange("p (c b s) -> p b c s", c=2, b=GB),
                                      q_half(HI, k).bitcast(F32), sub).then_inc(q_lo, 1)

            def s_biased(g, p, first):
                n = PAIRS * g + p
                dve.wait_ge(s_mm, n + 1)
                if p == 3:
                    dve.wait_ge(s_tr, n - 2)
                elif not first:
                    dve.wait_ge(s_tr, PAIRS * g)
                s = soft[:, p % 3, :]
                dve.tensor_tensor(s.rearrange("p (b n) -> p b n", b=2), sc[p % 2].rearrange("p (b n) -> p b n", b=2),
                                  kp("alibi").unsqueeze(1).to_broadcast((P, 2, GT)), add).then_inc(s_bias, 1)
                dve.wait_ge(s_bias, n + 1)
                dve.tensor_reduce(smx[:, p, :], heads(s), AX.X, ALU.max).then_inc(s_max, 1)

            def s_total(g, p):
                n = PAIRS * g + p
                dve.wait_ge(s_exp, n + 1)
                dve.tensor_reduce(ssum[:, p, :], heads(soft[:, p % 3, :]), AX.X, add).then_inc(s_sum, 1)
                dve.wait_ge(s_sum, n + 1)
                dve.reciprocal(srec[:, p, :], ssum[:, p, :]).then_inc(s_rec, 1)

            def s_transpose(g, p, first):
                n = PAIRS * g + p
                dve.wait_ge(s_norm, n + 1)
                if not first or p >= 2:
                    dve.wait_ge(p_lo, n - 1)
                dve.transpose(soft[:, 3 + p % 2, :], soft[:, p % 3, :]).then_inc(s_tr, 1)

            def probs_rest(g, p):
                dve.wait_ge(p_hi, PAIRS * g + p + 1)
                sl = [probsT[:, s, 2 * p:2 * p + 2].rearrange("p a b c -> p (a b c)") for s in (HI, LO)]
                dve.tensor_tensor(sl[LO], soft[:, 3 + p % 2, :], sl[HI].bitcast(F32), sub).then_inc(p_lo, 1)

            def o_rest(b):
                for q in range(NQ):
                    dve.wait_ge(o_hi, 2 * (NQ * b + q + 1))
                    for half in range(2):
                        dve.tensor_tensor(o_part(LO, half, q), av_part(half, q),
                                          o_part(HI, half, q).bitcast(F32), sub).then_inc(o_lo, 1)

            def attn_residual(b):
                for q in range(NQ):
                    dve.wait_ge(x1_in[q], 16 * (b + 1))
                    dve.wait_ge(wo_mm, NQ * b + q + 1)
                    dve.tensor_tensor(x1[:, q, :], row[q], x1[:, q, :], add).then_inc(x1_add, 1)

            def y_context(b, with_front):
                for q in range(NQ):
                    dve.wait_ge(y_mm, NQ * b + q + 1)
                    if with_front:
                        dve.wait_ge(c1_lo, 2 * (b + 2))
                        dve.wait_ge(v_ready, b + 2)
                    dve.tensor_tensor(
                        tmp[:, q, :].rearrange("p (b j) -> p b j", b=4), ybank[q].rearrange("p (b j) -> p b j", b=4),
                        ctxb[:, bass.ds(b * GB + 4 * q, 4)].unsqueeze(2).to_broadcast((P, 4, P)), add)\
                       .then_inc(y_t, 1)

            def y_rest(b):
                for q in range(NQ):
                    dve.wait_ge(yt_mm, NQ * b + q + 1)
                    dve.wait_ge(y_hi, NQ * b + q + 1)
                    dve.tensor_tensor(y_part(LO, q), yt_view(q), y_part(HI, q).bitcast(F32), sub).then_inc(y_lo, 1)
                    dve.tensor_reduce(ysum[:, :, 4 * q:4 * q + 4],
                                      ytbank[q].rearrange("p (b t o) -> p t b o", b=4, t=PH), AX.X, add)\
                       .then_inc(y_sum, 1)

            def coef_1(b):
                dve.wait_ge(co_mm, 2 * b + 1)
                dve.tensor_copy(co[:, 0, 0:GB], small[:, 0:GB]).then_inc(co_dve, 1)
                dve.wait_ge(co_dve, CO * b + 1)
                dve.tensor_tensor(co[:, 1, :].rearrange("p (b e) -> p b e", e=EXPERTS),
                                  co[:, 0, 0:GB].unsqueeze(2).to_broadcast((P, GB, EXPERTS)),
                                  kp("keysT").unsqueeze(1).to_broadcast((P, GB, EXPERTS)), mult)\
                   .then_inc(co_dve, 1)

            def coef_2(b):
                lg = small[:, 64:64 + GB * EXPERTS].rearrange("p (b e) -> p b e", e=EXPERTS)
                ex = co[:, 3, :].rearrange("p (b e) -> p b e", e=EXPERTS)
                dve.wait_ge(co_mm, 2 * b + 2)
                dve.tensor_reduce(comx[:, 0, :], lg, AX.X, ALU.max).then_inc(co_dve, 1)
                dve.wait_ge(co_dve, CO * b + 3)
                dve.tensor_tensor(co[:, 2, :].rearrange("p (b e) -> p b e", e=EXPERTS), lg,
                                  comx[:, 0, :].unsqueeze(2).to_broadcast((P, GB, EXPERTS)), sub)\
                   .then_inc(co_dve, 1)
                return ex

            def coef_3(b):
                ex = co[:, 3, :].rearrange("p (b e) -> p b e", e=EXPERTS)
                dve.wait_ge(co_exp, b + 1)
                dve.tensor_reduce(comx[:, 1, :], ex, AX.X, add).then_inc(co_dve, 1)
                dve.wait_ge(co_dve, CO * b + 5)
                dve.reciprocal(comx[:, 2, :], comx[:, 1, :]).then_inc(co_dve, 1)
                dve.wait_ge(co_dve, CO * b + 6)
                dve.tensor_tensor(ex, ex, comx[:, 2, :].unsqueeze(2).to_broadcast((P, GB, EXPERTS)), mult)\
                   .then_inc(co_dve, 1)
                dve.wait_ge(co_dve, CO * b + 7)
                pairs = co[:, 3, :].rearrange("p (b c e) -> p c b e", c=EXPERTS // 2, e=2)
                dve.tensor_scalar(coef[:, 0], pairs[:, :, :, 0], kp("even"), None, mult).then_inc(co_dve, 1)
                dve.wait_ge(co_dve, CO * b + 8)
                dve.scalar_tensor_tensor(out=coef[:, 1], in0=pairs[:, :, :, 1], scalar=kp("odd"),
                                         in1=coef[:, 0], op0=mult, op1=add).then_inc(co_dve, 1)

            def hidden(b):
                for k in range(2):
                    dve.wait_ge(h_mm, 2 * b + k + 1)
                    dve.wait_ge(co_dve, CO * (b + 1))
                    dve.wait_ge(yt_mm, NQ * b + k + 1)
                    dve.tensor_tensor(
                        tmp[:, k, :].rearrange("p (e s b) -> p e s b", s=SEQ, b=4),
                        feat[k].rearrange("p (e s b) -> p e s b", s=SEQ, b=4),
                        coef[:, 1, 2 * k:2 * k + 2, :].rearrange("p e (q b) -> p (e q) b", b=4).unsqueeze(2)
                        .to_broadcast((P, 2 * NQ, SEQ, 4)), mult)\
                       .then_inc(h_t, 1)

            def out_residual(b):
                for q in range(NQ):
                    dve.wait_ge(out_mm, NQ * b + q + 1)
                    dve.wait_ge(xph_in[q], 16 * (b + 1))
                    dve.tensor_tensor(x1[:, q, :], row[q], x1[:, q, :], add).then_inc(out_add, 1)

            c1_bias(0, True)
            kv(0)
            q_rest(0)
            s_biased(0, 0, True)
            s_biased(0, 1, True)
            s_total(0, 0)
            s_biased(0, 2, True)
            s_total(0, 1)
            s_transpose(0, 0, True)
            s_biased(0, 3, True)
            s_total(0, 2)
            s_transpose(0, 1, True)
            probs_rest(0, 0)
            s_total(0, 3)
            s_transpose(0, 2, True)
            probs_rest(0, 1)
            s_transpose(0, 3, True)
            probs_rest(0, 2)
            probs_rest(0, 3)
            mix_reduce(1, False)

            def body(g, last):
                o_rest(g - 1)
                c1_bias(g, False)
                attn_residual(g - 1)
                kv(g)
                q_rest(g)
                y_context(g - 1, True)
                s_biased(g, 0, False)
                s_biased(g, 1, False)
                y_rest(g - 1)
                s_biased(g, 2, False)
                s_total(g, 0)
                coef_1(g - 1)
                s_total(g, 1)
                s_transpose(g, 0, False)
                s_biased(g, 3, False)
                coef_2(g - 1)
                s_transpose(g, 1, False)
                s_total(g, 2)
                coef_3(g - 1)
                hidden(g - 1)
                probs_rest(g, 0)
                probs_rest(g, 1)
                s_total(g, 3)
                s_transpose(g, 2, False)
                s_transpose(g, 3, False)
                probs_rest(g, 2)
                probs_rest(g, 3)
                if not last:
                    mix_reduce(g + 1, False)
                out_residual(g - 1)

            with dve.Fori(1, GROUPS - 1) as g:
                body(g, False)
            body(GROUPS - 1, True)
            b = GROUPS - 1
            o_rest(b)
            attn_residual(b)
            y_context(b, False)
            y_rest(b)
            coef_1(b)
            coef_2(b)
            coef_3(b)
            hidden(b)
            out_residual(b)


def kernel(**inputs):
    import numpy as np
    import concourse.bacc as bacc
    from concourse.bass_utils import run_bass_kernel_spmd

    a = {k: np.asarray(v) for k, v in inputs.items()}
    f32 = np.float32
    J = DIM // PH

    def by_phase(rows):
        return rows.reshape(J, PH, -1)

    def cols_by_phase(m):
        return m.reshape(m.shape[0], J, PH).transpose(0, 2, 1).reshape(m.shape[0], DIM)

    def spread_rows(m, n=P):
        return np.broadcast_to(m.reshape(1, -1), (n, m.size))

    x = a["x"].reshape(BATCH // 4, 4, SEQ, DIM).transpose(0, 2, 1, 3).reshape(TOK, DIM)
    x = np.ascontiguousarray(cols_by_phase(x))

    wo = a["L0_attn_Wo"].reshape(4, 2, 4, HD, DIM).transpose(1, 0, 3, 2, 4)
    down = a["L0_ffn_lora_down"].transpose(1, 0, 2).reshape(DIM, EXPERTS * RANK)
    up = a["L0_ffn_lora_up"].reshape(PH, P, DIM).transpose(1, 0, 2)
    weights = {
        "wq": by_phase(a["L0_attn_Wq"]),
        "wo": cols_by_phase(np.ascontiguousarray(wo).reshape(-1, DIM)),
        "wd": by_phase(down),
        "worg": by_phase(cols_by_phase(np.ascontiguousarray(a["L0_ffn_W_org"].T))),
        "wu": cols_by_phase(np.ascontiguousarray(up).reshape(-1, DIM)),
    }
    weights = {k: np.ascontiguousarray(v.reshape(P, PH * DIM)) for k, v in weights.items()}

    conv_w = a["L0_cond2_weight"]
    width, taps = conv_w.shape[1], conv_w.shape[2]
    wconv = np.zeros((PH, SEQ, 3, PH, SEQ), f32)
    for r in range(PH):
        for tap in range(taps):
            m = r + tap - taps // 2
            for o in range(SEQ):
                i0 = o // width * width
                wconv[m % PH, i0:i0 + width, m // PH + 1, r, o] = conv_w[o, :, tap]
    kvc = np.concatenate([by_phase(a["L0_attn_Wkv"]).reshape(P, -1), wconv.reshape(P, -1)], axis=1)

    p = np.arange(P)
    first = 2.0 ** (-2.0 ** (-(np.log2(HEADS) - 3)))
    slopes = np.array([first ** (i + 1) for i in range(HEADS)], dtype=f32)
    pos = np.arange(SEQ)
    far = (pos[None, :] - pos[:, None]).astype(f32)
    alibi = slopes.reshape(4, 1, HC, 1) * far[None, :, None, :]
    alibi = np.where((far <= 0)[None, :, None, :], alibi, f32(-1e30)).astype(f32).reshape(P, HC * SEQ)
    kernels = a["L0_cond_weight"][..., 0]
    bank_bias = np.zeros((SEQ, 4, 4, SEQ), f32)
    for b in range(4):
        bank_bias[0:MIX, b, b, :] = a["L0_cond_bias_k"]

    sel = np.zeros((P, P), f32)
    sel[0:BATCH] = np.arange(BATCH)[:, None] % 4 == p[None, :] % 4
    qmask = np.zeros((P, BATCH // 4), f32)
    qmask[0:BATCH] = np.arange(BATCH)[:, None] // 4 == np.arange(BATCH // 4)[None, :]

    start = dict(
        sel=sel, qmask=qmask, condT=a["cond_128"].T, w0=a["L0_cond_W0"], w1=a["L0_cond_W1"], w2=a["L0_cond_W2"],
        b0=a["L0_cond_b0"].reshape(P, 1), b1=a["L0_cond_b1"].reshape(P, 1), b2=spread_rows(a["L0_cond_b2"]),
        bank_bias=bank_bias.reshape(P, P),
        bank_w=np.repeat(kernels.transpose(2, 1, 0).reshape(SEQ, SEQ * MIX), 4, axis=0),
        kdiag=(p[:, None] // 4 == np.arange(MIX)[None, :]).astype(f32),
        cwT=np.tile(a["L0_cond2_c_weight"].T, (1, PH)), fside=np.tile(a["fside_S_0"], PH).reshape(P, 1))
    keep = dict(
        alibi=alibi, kvscale=np.where(p % 32 < HD, HD ** -0.5, 1.0).astype(f32).reshape(P, 1),
        quad=(p[:, None] // 32 == np.arange(4)[None, :]).astype(f32),
        lane=(p[:, None] % 4 == np.arange(4)[None, :]).astype(f32),
        even=(p < RANK).astype(f32).reshape(P, 1), odd=(p >= RANK).astype(f32).reshape(P, 1),
        keysT=a["L0_ffn_lora_keys"].T,
        wq2=by_phase(np.ascontiguousarray(a["L0_ffn_Wq"].T)).reshape(P, -1), ones=np.ones((P, P), f32),
        ident=np.eye(P, dtype=f32))
    arrays = {
        "x": x,
        "start": np.concatenate([start[n] for n in START], axis=1),
        "keep": np.concatenate([keep[n] for n in KEEP], axis=1),
        "kvc": kvc, **weights,
    }
    arrays = {f"in_{k}": np.ascontiguousarray(v) for k, v in arrays.items()}

    nc = bacc.Bacc("TRN2", target_bir_lowering=False, num_devices=1)
    d = {k: nc.dram_tensor(k, v.shape, F32, kind="ExternalInput").ap() for k, v in arrays.items()}
    out = nc.dram_tensor("out", (TOK, DIM), F32, kind="ExternalOutput").ap()
    swap = nc.dram_tensor("swap", (NQ, PH, SEQ, 4, J), F32, kind="Internal").ap()
    build(nc, d["in_x"], d["in_start"], d["in_keep"], d["in_kvc"], {n: d[f"in_{n}"] for n in WEIGHTS}, swap, out)
    r = run_bass_kernel_spmd(nc, [arrays], core_ids=[0])
    got = r.results[0]["out"]
    got = got.reshape(BATCH // 4, SEQ, 4, PH, J).transpose(0, 2, 1, 4, 3)
    return np.ascontiguousarray(got).reshape(BATCH, SEQ, DIM)
```

```python
import concourse.bass as bass
from concourse import mybir
from contextlib import ExitStack

F32 = mybir.dt.float32
F32R = mybir.dt.float32r
ALU = mybir.AluOpType
ACT = mybir.ActivationFunctionType
AX = mybir.AxisListType

P = 128
BATCH, SEQ, DIM = 64, 32, 512
TOK = BATCH * SEQ
GROUPS = 8
GT = TOK // GROUPS
GB = GT // SEQ
NQ = GT // P
PH = DIM // P
HEADS, HD = 32, 16
HC = P // HD
PAIRS = GB // 2
EXPERTS, RANK = 8, 64
MIX = 8
HI, LO = 0, 1

START = dict(sel=128, qmask=16, condT=64, w0=128, w1=128, w2=8, b0=1, b1=1, b2=8, bank_bias=128, bank_w=256, kdiag=8,
             cwT=128, fside=1)
KEEP = dict(alibi=256, kvscale=1, quad=4, lane=4, keysT=8, wq2=512, ones=128, ident=128)


def columns(pack):
    at, out = 0, {}
    for name, n in pack.items():
        out[name] = (at, at + n)
        at += n
    return out, at


START_AT, START_N = columns(START)
KEEP_AT, KEEP_N = columns(KEEP)
WEIGHTS = ["wq", "wo", "wd", "worg", "wu"]


def build(nc, x_d, start_d, keep_d, kvc_d, w_d, swap_d, out_d):
    ctx = ExitStack()
    with ctx:
        def sb(name, shape, dt=F32):
            return ctx.enter_context(nc.sbuf_tensor(name, shape, dt))

        def sem(name):
            return ctx.enter_context(nc.semaphore(name))

        W = {n: sb(n, [P, 2, PH, DIM], F32R) for n in WEIGHTS}
        wkv = sb("wkv", [P, 2, PH, 4, 2 * HD], F32R)
        wconv = sb("wconv", [P, 2, 3, P], F32R)
        keep = sb("keep", [P, KEEP_N])
        c1_y = sb("c1_y", [P, 2, PH, GT], F32R)
        o_h = sb("o_h", [P, 2, PH, GT], F32R)
        q_x = sb("q_x", [P, 2, PH * GT], F32R)
        kdiag = sb("kdiag", [P, 2, HC, GT], F32R)
        vdiag = sb("vdiag", [P, 2, GB, 2, 4, HD], F32R)
        probsT = sb("probsT", [P, 2, GB, HC, SEQ], F32R)
        xphase = sb("xphase", [P, 2, GB, P + 2], F32R)
        staging = sb("staging", [P, 3, DIM])
        xin = sb("xin", [P, NQ * DIM])
        x1 = sb("x1", [P, NQ, DIM])
        tmp = sb("tmp", [P, 2, DIM])
        soft = sb("soft", [P, 5, DIM])
        aggb = sb("aggb", [P, TOK])
        ctxb = sb("ctxb", [P, BATCH])
        mixd = sb("mixd", [P, 2, NQ, 4, SEQ], F32R)
        mix_att = sb("mix_att", [P, BATCH // 4, MIX])
        mix_a = sb("mix_a", [P, NQ, SEQ])
        mix_hl = sb("mix_hl", [P, 2, NQ, SEQ], F32R)
        smx = sb("smx", [P, PAIRS, 2 * HC])
        ssum = sb("ssum", [P, PAIRS, 2 * HC])
        srec = sb("srec", [P, PAIRS, 2 * HC])
        ysum = sb("ysum", [P, PH, GB])
        co = sb("co", [P, 4, GB * EXPERTS])
        expert_w = sb("expert_w", [P, PH, EXPERTS])
        comx = sb("comx", [P, 3, GB])
        coef = sb("coef", [P, EXPERTS // 2, GB])
        attd = sb("attd", [P, BATCH // 4])
        mixs = sb("mixs", [P, 24])
        keep_bank = sb("keep_bank", [P, SEQ * MIX])
        hmlp = aggb[:, 0:2 * BATCH].rearrange("p (a b) -> p a b", a=2)
        diag_att = aggb[:, DIM:DIM + BATCH // 4 * MIX]
        start = soft[:, 3:5, :].rearrange("p a b -> p (a b)")

        def st(name):
            a, b = START_AT[name]
            return start[:, a:b]

        def kp(name):
            a, b = KEEP_AT[name]
            return keep[:, a:b]

        def q_half(s, k):
            return q_x[:, s, :].rearrange("p (b c s) -> p b c s", b=GB, c=PH)[:, :, 2 * k:2 * k + 2, :]

        def av_part(half, q):
            return avbank[q][0:64].rearrange("p a (b h s) -> p (a b) h s", b=2, h=HC)[:, :, 4 * half:4 * half + 4]

        def is_last(b):
            return isinstance(b, int) and b == GROUPS - 1

        def o_of(b):
            return q_x[:].rearrange("p s (c n) -> p s c n", c=PH) if is_last(b) else o_h

        def x_of(g):
            return o_h[:].rearrange("p s c n -> p s (c n)") if isinstance(g, int) and g == 1 else q_x

        def x1_of(b):
            return staging if is_last(b) else x1

        def attn_row(b, q):
            return sc[q] if is_last(b) else row[q]

        def o_part(b, s, half, q):
            return o_of(b)[64 * half:64 * half + 64, s, :, q * P:(q + 1) * P].rearrange("p h (s b) -> p b h s", b=4)

        def yt_view(q):
            return ytbank[q].rearrange("p (b t o) -> p b t o", b=4, t=PH)

        def y_part(s, q):
            return c1_y[:, s, :, q * P:(q + 1) * P].rearrange("p t (o b) -> p b t o", b=4)

        ones = kp("ones")
        expert_prod = kp("wq2")[:, 0:PH * GB * EXPERTS]
        kvt = tmp[:, 0, 0:GT]
        kv_hl = soft[:, 3, :].bitcast(F32R).rearrange("p (s n) -> p s n", s=2)
        vnat = tmp[:, 1, :]
        kv_in = tmp[:, 0, 0:128].rearrange("p (t n) -> p t n", t=PH)

        def pb(name, banks=1):
            return ctx.enter_context(nc.psum_tensor(name, [P, banks, DIM], F32))

        feat, score, aux = pb("feat", 2), pb("score", 2), pb("aux", 2)
        rows = [pb(f"rows{q}") for q in range(NQ)]
        feat, sc = [feat[:, k, :] for k in range(2)], [score[:, k, :] for k in range(2)]
        row = [r[:, 0, :] for r in rows]
        small = aux[:, 1, :]
        ybank = [aux[:, 0, :], feat[0]]
        ytbank = [feat[1], aux[:, 0, :]]
        avbank = [score, aux]

        start_in, keep_in, kvc_in = sem("start_in"), sem("keep_in"), sem("kvc_in")
        stage_in = [sem(f"stage_in{u}") for u in range(7)]
        x_in, x1_in = sem("x_in"), [sem(f"x1_in{q}") for q in range(NQ)]
        k_spread = sem("k_spread")
        xph_in = [sem(f"xph_in{q}") for q in range(NQ)]
        out_done = [sem(f"out_done{q}") for q in range(NQ)]
        zeroed, wu_lo, expert_mm, expert_done = sem("zeroed"), sem("wu_lo"), sem("expert_mm"), sem("expert_done")
        w_hi, w_lo, kvc_hi, kvc_lo = sem("w_hi"), sem("w_lo"), sem("kvc_hi"), sem("kvc_lo")
        mlp_mm, mlp_act, mixs_dve, mixs_exp, bank_kept = (sem("mlp_mm"), sem("mlp_act"), sem("mixs_dve"),
                                                          sem("mixs_exp"), sem("bank_kept"))
        ctx_mm, ctx_done = sem("ctx_mm"), sem("ctx_done")
        agg_outer, agg_mm, agg_done = sem("agg_outer"), sem("agg_mm"), sem("agg_done")
        mix_prod, mix_red, mix_split, mix_ready = (sem("mix_prod"), sem("mix_red"), sem("mix_split"),
                                                   sem("mix_ready"))
        x_hi, x_lo = sem("x_hi"), sem("x_lo")
        c1_mm, c1_t, c1_hi, c1_lo = sem("c1_mm"), sem("c1_t"), sem("c1_hi"), sem("c1_lo")
        kv_mm, kv_t, kv_hi, kv_lo, v_tr, v_ready = (sem("kv_mm"), sem("kv_t"), sem("kv_hi"), sem("kv_lo"),
                                                    sem("v_tr"), sem("v_ready"))
        q_mm, q_hi, q_lo = sem("q_mm"), sem("q_hi"), sem("q_lo")
        s_mm, s_bias, s_max, s_sub, s_exp, s_sum, s_rec, s_norm, s_tr, p_hi, p_lo01, p_lo23 = (
            sem("s_mm"), sem("s_bias"), sem("s_max"), sem("s_sub"), sem("s_exp"), sem("s_sum"),
            sem("s_rec"), sem("s_norm"), sem("s_tr"), sem("p_hi"), sem("p_lo01"), sem("p_lo23"))
        av_mm, o_hi, o_lo = sem("av_mm"), sem("o_hi"), sem("o_lo")
        wo_mm, x1_add = sem("wo_mm"), sem("x1_add")
        xph_hi, xph_lo = sem("xph_hi"), sem("xph_lo")
        y_mm, y_t, yt_mm = sem("y_mm"), [sem(f"y_t{q}") for q in range(NQ)], sem("yt_mm")
        y_sum, y_hi, y_lo = sem("y_sum"), sem("y_hi"), sem("y_lo")
        co_mm, co_dve, co_exp = sem("co_mm"), sem("co_dve"), sem("co_exp")
        h_mm, h_t, h_hi, h_lo = sem("h_mm"), sem("h_t"), sem("h_hi"), sem("h_lo")
        out_mm, out_add = sem("out_mm"), sem("out_add")

        swap_out = [sem(f"swap_out{q}") for q in range(NQ)]
        swap_rows = [swap_d[q].rearrange("t i m j -> (i m) t j") for q in range(NQ)]
        swap_cols = [swap_d[q].rearrange("t i m j -> (t i) (m j)") for q in range(NQ)]

        x_g = x_d.rearrange("(g q p) c -> p g q c", q=NQ, p=P)
        out_g = out_d.rearrange("(g q p) c -> p g q c", q=NQ, p=P)

        NW = len(WEIGHTS) * PH
        SLOT = [n % 5 for n in range(NW)]
        SLOT[17:20] = [5, 6, 2]
        X1_FREE = 15

        LAST_LO = 17

        def stage(n):
            u = SLOT[n]
            return staging[:, u, :] if u < 3 else x1[:, u - 3, :] if u < 5 else tmp[:, u - 5, :]

        def uses(n):
            before = [m for m in range(n) if SLOT[m] == SLOT[n]]
            return len(before) + 1, (before[-1] if before else None)

        NB4 = BATCH // 4
        CO = 8

        block = ctx.enter_context(nc.Block())

        @block.sync
        def _(sp):
            sp.dma_start(start[:, 0:START_N], start_d).then_inc(start_in, 16)

            def load_weight(n):
                before = uses(n)[1]
                if before is not None:
                    sp.wait_ge(w_hi, before + 1)
                    sp.wait_ge(w_lo, before + 1)
                name, c = WEIGHTS[n // PH], n % PH
                sp.dma_start(stage(n), w_d[name][:, c * DIM:(c + 1) * DIM]).then_inc(stage_in[SLOT[n]], 16)

            def spread_k(g, h):
                sp.wait_ge(kv_hi, g + 1)
                sp.wait_ge(kv_lo, g + 1)
                src = 32 * (h % 4)
                sp.dma_start(kdiag[HD * h:HD * (h + 1), :, h, :].bitcast(F32),
                             kv_hl[src:src + HD, :, :].bitcast(F32)).then_inc(k_spread, 16)

            def load_x(g):
                sp.dma_start(xin[:].rearrange("p (q c) -> p q c", q=NQ),
                             x_g[:, bass.ds(g, 1)].squeeze(1)).then_inc(x_in, 16)

            def load_x1(g, q):
                sp.dma_start(x1_of(g)[:, q, :], x_g[:, bass.ds(g, 1), q].squeeze(1)).then_inc(x1_in[q], 16)

            def by_phase(b, g=None):
                def write(q):
                    sp.wait_ge(x1_add, NQ * b + q + 1)
                    sp.dma_start(swap_rows[q], x1_of(b)[:, q, :].rearrange("p (t j) -> p t j", t=PH))\
                      .then_inc(swap_out[q], 16)

                def read(q):
                    sp.wait_ge(swap_out[q], 16 * (b + 1))
                    sp.dma_start(xin[:, q * DIM:(q + 1) * DIM], swap_cols[q]).then_inc(xph_in[q], 16)

                if g is None:
                    write(0)
                    write(1)
                    read(0)
                    read(1)
                else:
                    write(0)
                    write(1)
                    read(0)
                    read(1)
                    spread_k(g, 2)
                    spread_k(g, 6)
                    spread_k(g, 1)
                    spread_k(g, 4)
                    spread_k(g, 7)
                    spread_k(g, 0)
                    spread_k(g, 5)
                    spread_k(g, 3)

            def store(b, last):
                for q in range(NQ):
                    sp.wait_ge(out_add, NQ * b + q + 1)
                    sp.dma_start(out_g[:, bass.ds(b, 1), q].squeeze(1), x1_of(b)[:, q, :]).then_inc(out_done[q], 16)
                for q in range(NQ):
                    sp.wait_ge(out_done[q], 16 * (b + 1))
                    if not last:
                        load_x1(b + 1, q)

            for n in range(7):
                load_weight(n)
            sp.wait_ge(x_hi, 1)
            sp.wait_ge(x_lo, NQ)
            load_x(1)
            for n in range(7, 14):
                load_weight(n)
            sp.wait_ge(zeroed, 3)
            for h in range(HC):
                spread_k(0, h)
            for n in range(14, 17):
                load_weight(n)
            sp.wait_ge(mix_red, 2)
            for n in range(17, NW):
                load_weight(n)
            sp.wait_ge(w_hi, X1_FREE)
            sp.wait_ge(w_lo, X1_FREE)
            for q in range(NQ):
                load_x1(0, q)

            with sp.Fori(1, GROUPS - 1) as g:
                by_phase(g - 1, g)
                sp.wait_ge(xph_hi, NQ * g)
                sp.wait_ge(xph_lo, NQ * g)
                load_x(g + 1)
                store(g - 1, False)
            by_phase(GROUPS - 2, GROUPS - 1)
            sp.wait_ge(mix_red, GROUPS)
            for q in range(NQ):
                load_x1(GROUPS - 1, q)
            sp.wait_ge(xph_hi, NQ * (GROUPS - 1))
            sp.wait_ge(xph_lo, NQ * (GROUPS - 1))
            by_phase(GROUPS - 1)
            store(GROUPS - 2, True)
            store(GROUPS - 1, True)

        @block.tensor
        def _(pe):
            def split_mm(out, a_hi, a_lo, b_hi, b_lo, first, last):
                pe.matmul(out, a_hi, b_hi, start=first, stop=False)
                pe.matmul(out, a_hi, b_lo, start=False, stop=False)
                return pe.matmul(out, a_lo, b_hi, start=False, stop=last)

            def warm(n):
                for _ in range(n):
                    pe.matmul(row[1][:, 0:GT], ones, kp("alibi"), start=True, stop=True)

            pe.wait_ge(start_in, 16)
            pe.matmul(small[:, 0:BATCH], st("w0"), st("condT"), start=True, stop=True).then_inc(mlp_mm, 1)
            pe.matmul(sc[0][:, 0:BATCH], st("cwT"), st("condT"), start=True, stop=True).then_inc(ctx_mm, 1)
            pe.wait_ge(mlp_act, 1)
            pe.matmul(small[:, 0:BATCH], st("w1"), hmlp[:, 0, :], start=True, stop=True).then_inc(mlp_mm, 1)
            pe.wait_ge(mlp_act, 2)
            pe.matmul(small[0:BATCH, 0:MIX], hmlp[:, 1, :], st("w2"), start=True, stop=True).then_inc(mlp_mm, 1)

            pe.wait_ge(keep_in, 16)
            for t in range(PH):
                mm = pe.matmul(row[0][:, t * EXPERTS:(t + 1) * EXPERTS], kp("wq2")[:, t * P:(t + 1) * P], kp("keysT"),
                               start=True, stop=True)
            mm.then_inc(expert_mm, 1)
            warm(4)

            pe.wait_ge(mixs_dve, 7)
            pe.matmul(small[:, 0:NB4 * MIX], st("sel")[0:BATCH, :], diag_att[0:BATCH, :],
                      start=True, stop=True).then_inc(mlp_mm, 1)
            warm(2)

            def agg_part(c):
                pe.wait_ge(agg_outer, c + 1)
                if c == 0:
                    pe.wait_ge(keep_in, 16)
                    pe.wait_ge(ctx_done, 1)
                if c >= 2:
                    pe.wait_ge(agg_done, c - 1)
                pe.matmul(sc[c % 2], ones, aggb[:, c * DIM:(c + 1) * DIM], start=True, stop=True).then_inc(agg_mm, 1)

            def mix(g):
                pe.wait_ge(x_hi, g + 1)
                pe.wait_ge(x_lo, NQ * (g + 1))
                pe.wait_ge(mix_ready, g + 1)
                for k in range(2):
                    for t in range(2 * k, 2 * k + 2):
                        for q in range(NQ):
                            at = (t % 2) * GT + q * P
                            xs = [x_of(g)[:, s, q * DIM + t * P:q * DIM + (t + 1) * P] for s in (HI, LO)]
                            ms = [mixd[:, s, q].rearrange("p a b -> p (a b)") for s in (HI, LO)]
                            mm = split_mm(feat[k][:, at:at + P], xs[HI], xs[LO], ms[HI], ms[LO], True, True)
                    mm.then_inc(c1_mm, 1)

            def kv(g):
                pe.wait_ge(kvc_hi, 1)
                pe.wait_ge(kvc_lo, 1)
                for t in range(PH):
                    if t % 2 == 0:
                        pe.wait_ge(c1_hi, 2 * g + t // 2 + 1)
                        pe.wait_ge(c1_lo, 2 * g + t // 2 + 1)
                    ws = [wkv[:, s, t].rearrange("p r n -> p (r n)") for s in (HI, LO)]
                    mm = split_mm(small[:, 0:GT], ws[HI], ws[LO], c1_y[:, HI, t, :], c1_y[:, LO, t, :],
                                  t == 0, t == PH - 1)
                mm.then_inc(kv_mm, 1)

            def queries(g):
                pe.wait_ge(w_hi, PH)
                pe.wait_ge(w_lo, PH)
                for c in range(PH):
                    for t in range(PH):
                        ws = [W["wq"][:, s, t, c * P:(c + 1) * P] for s in (HI, LO)]
                        at = (c % 2) * GT
                        mm = split_mm(feat[c // 2][:, at:at + GT], ws[HI], ws[LO],
                                      c1_y[:, HI, t, :], c1_y[:, LO, t, :], t == 0, t == PH - 1)
                    if c % 2:
                        mm.then_inc(q_mm, 1)

            def scores(g, p):
                if p == 0:
                    pe.wait_ge(q_hi, 2 * (g + 1))
                    pe.wait_ge(q_lo, 2 * (g + 1))
                    pe.wait_ge(k_spread, 16 * HC * (g + 1))
                if p >= 2:
                    pe.wait_ge(s_bias, PAIRS * g + p - 1)
                for b in (2 * p, 2 * p + 1):
                    qs = [q_x[:, s, b * P:(b + 1) * P] for s in (HI, LO)]
                    ks = [kdiag[:, s, :, b * SEQ:(b + 1) * SEQ] for s in (HI, LO)]
                    at = (b % 2) * GT
                    mm = split_mm(sc[p % 2][:, at:at + GT], qs[HI], qs[LO], ks[HI], ks[LO], True, True)
                mm.then_inc(s_mm, 1)

            def attend(b, q):
                pe.wait_ge(v_ready, b + 1)
                pe.wait_ge(p_hi, PAIRS * b + 2 * q + 2)
                pe.wait_ge(p_lo01 if q == 0 else p_lo23, 2 * (b + 1))
                for m in range(4):
                    n = 4 * q + m
                    vs = [vdiag[:, s, n].rearrange("p z c d -> p (z c d)") for s in (HI, LO)]
                    ps = [probsT[:, s, n].rearrange("p a b -> p (a b)") for s in (HI, LO)]
                    mm = split_mm(avbank[q][:, m // 2, m % 2 * GT:(m % 2 + 1) * GT],
                                  vs[HI], vs[LO], ps[HI], ps[LO], True, True)
                mm.then_inc(av_mm, 1)

            def out_proj(b, q):
                pe.wait_ge(w_hi, 2 * PH)
                pe.wait_ge(w_lo, 2 * PH)
                pe.wait_ge(o_hi, 2 * (NQ * b + q + 1))
                pe.wait_ge(o_lo, 2 * (NQ * b + q + 1))
                for c in range(PH):
                    os = [o_of(b)[:, s, c, q * P:(q + 1) * P] for s in (HI, LO)]
                    mm = split_mm(attn_row(b, q), os[HI], os[LO], W["wo"][:, HI, c, :], W["wo"][:, LO, c, :],
                                  c == 0, c == PH - 1)
                mm.then_inc(wo_mm, 1)

            def conv(b, q, with_front):
                pe.wait_ge(xph_hi, NQ * b + q + 1)
                pe.wait_ge(xph_lo, NQ * b + q + 1)
                if q == 1 and with_front:
                    pe.wait_ge(q_hi, 2 * (b + 1) + 1)
                    pe.wait_ge(q_lo, 2 * (b + 1) + 1)
                for k in range(3):
                    xs = [xphase[:, s, 4 * q:4 * q + 4, k:k + P] for s in (HI, LO)]
                    mm = split_mm(ybank[q], wconv[:, HI, k, :], wconv[:, LO, k, :], xs[HI], xs[LO],
                                  k == 0, k == 2)
                mm.then_inc(y_mm, 1)

            def transpose_y(b, q, with_front):
                pe.wait_ge(y_t[q], b + 1)
                if q == 0 and with_front:
                    pe.wait_ge(q_lo, 2 * (b + 1) + 2)
                for m in range(4):
                    mm = pe.transpose(ytbank[q][:, m * P:(m + 1) * P], tmp[:, q, m * P:(m + 1) * P], kp("ident"))
                mm.then_inc(yt_mm, 1)

            def coef_scores(b):
                pe.wait_ge(co_dve, CO * b + 2)
                pe.matmul(small[:, 0:GB * EXPERTS], ones, co[:, 0, :], start=True, stop=True).then_inc(co_mm, 1)

            def lora_down(b, k):
                pe.wait_ge(w_hi, 3 * PH)
                pe.wait_ge(w_lo, 3 * PH)
                pe.wait_ge(y_hi, NQ * (b + 1))
                pe.wait_ge(y_lo, NQ * (b + 1))
                for e in (2 * k, 2 * k + 1):
                    for t in range(PH):
                        ws = [W["wd"][:, s, t, e * P:(e + 1) * P] for s in (HI, LO)]
                        at = (e % 2) * GT
                        mm = split_mm(feat[k][:, at:at + GT], ws[HI], ws[LO],
                                      c1_y[:, HI, t, :], c1_y[:, LO, t, :], t == 0, t == PH - 1)
                mm.then_inc(h_mm, 1)

            def base(b, q):
                if q == 0:
                    pe.wait_ge(w_hi, 4 * PH)
                    pe.wait_ge(w_lo, 4 * PH)
                pe.wait_ge(y_hi, NQ * b + q + 1)
                pe.wait_ge(y_lo, NQ * b + q + 1)
                if is_last(b):
                    pe.wait_ge(out_add, NQ * b)
                for t in range(PH):
                    ys = [c1_y[:, s, t, q * P:(q + 1) * P] for s in (HI, LO)]
                    split_mm(row[q], ys[HI], ys[LO], W["worg"][:, HI, t, :], W["worg"][:, LO, t, :],
                             t == 0, False)

            def lora_up(b):
                pe.wait_ge(w_hi, NW)
                pe.wait_ge(w_lo, LAST_LO)
                pe.wait_ge(wu_lo, NW - LAST_LO)
                for k in range(2):
                    pe.wait_ge(h_hi, 2 * b + k + 1)
                    pe.wait_ge(h_lo, 2 * b + k + 1)
                    for q in range(NQ):
                        for e in (2 * k, 2 * k + 1):
                            hs = [o_h[:, s, e, q * P:(q + 1) * P] for s in (HI, LO)]
                            mm = split_mm(row[q], hs[HI], hs[LO], W["wu"][:, HI, e, :], W["wu"][:, LO, e, :],
                                          False, e == PH - 1)
                        if k == 1:
                            mm.then_inc(out_mm, 1)

            agg_part(0)
            mix(0)
            kv(0)
            queries(0)
            for c in range(1, 4):
                agg_part(c)
            pe.wait_ge(zeroed, 3)
            pe.wait_ge(agg_done, 4)
            for p in range(PAIRS):
                scores(0, p)
            mix(1)
            pe.wait_ge(s_max, 3)
            warm(10)

            def front_and_back(g, mixed=False):
                b = g - 1
                attend(b, 0)
                if not mixed:
                    mix(g)
                attend(b, 1)
                out_proj(b, 0)
                out_proj(b, 1)
                kv(g)
                queries(g)
                conv(b, 0, True)
                conv(b, 1, True)
                transpose_y(b, 0, True)
                scores(g, 0)
                transpose_y(b, 1, True)
                scores(g, 1)
                base(b, 0)
                scores(g, 2)
                base(b, 1)
                scores(g, 3)
                coef_scores(b)
                lora_down(b, 0)
                lora_down(b, 1)

            front_and_back(1, mixed=True)
            lora_up(0)
            with pe.Fori(2, GROUPS - 1) as g:
                front_and_back(g)
                lora_up(g - 1)
            front_and_back(GROUPS - 1)
            b = GROUPS - 1
            attend(b, 0)
            attend(b, 1)
            out_proj(b, 0)
            out_proj(b, 1)
            lora_up(b - 1)
            conv(b, 0, False)
            conv(b, 1, False)
            transpose_y(b, 0, False)
            transpose_y(b, 1, False)
            base(b, 0)
            base(b, 1)
            coef_scores(b)
            lora_down(b, 0)
            lora_down(b, 1)
            lora_up(b)

        @block.scalar
        def _(act):
            def copy(out, in_):
                return act.activation(out, in_, ACT.Copy)

            act.dma_start(xin[:].rearrange("p (q c) -> p q c", q=NQ), x_g[:, 0]).then_inc(x_in, 16)
            act.dma_start(tmp[:, 0, :], kvc_d).then_inc(kvc_in, 16)
            act.dma_start(keep[:], keep_d).then_inc(keep_in, 16)

            def split_weight(n):
                act.wait_ge(stage_in[SLOT[n]], 16 * uses(n)[0])
                copy(W[WEIGHTS[n // PH]][:, HI, n % PH, :], stage(n)).then_inc(w_hi, 1)

            def x_split(g):
                act.wait_ge(x_in, 16 * (g + 1))
                copy(x_of(g)[:, HI, :], xin[:]).then_inc(x_hi, 1)

            def aggb_copy(c):
                act.wait_ge(agg_mm, c + 1)
                copy(aggb[:, c * DIM:(c + 1) * DIM], sc[c % 2]).then_inc(agg_done, 1)

            def c1_split(g):
                for k in range(2):
                    act.wait_ge(c1_t, 2 * g + k + 1)
                    copy(c1_y[:, HI, 2 * k:2 * k + 2, :].rearrange("p a b -> p (a b)"),
                         tmp[:, k, :]).then_inc(c1_hi, 1)

            def kv_split(g):
                act.wait_ge(kv_t, g + 1)
                copy(kv_hl[:, HI, :], kvt).then_inc(kv_hi, 1)

            def q_split(g, k):
                act.wait_ge(q_mm, 2 * g + k + 1)
                copy(q_half(HI, k), feat[k].rearrange("p (c b s) -> p b c s", c=2, b=GB)).then_inc(q_hi, 1)

            def exp(g, p):
                act.wait_ge(s_sub, PAIRS * g + p + 1)
                act.activation(soft[:, p % 3, :], soft[:, p % 3, :], ACT.Exp).then_inc(s_exp, 1)

            def probs_split(g, p):
                act.wait_ge(s_tr, PAIRS * g + p + 1)
                copy(probsT[:, HI, 2 * p:2 * p + 2].rearrange("p a b c -> p (a b c)"),
                     soft[:, 3 + p % 2, :]).then_inc(p_hi, 1)

            def o_split(b, q):
                act.wait_ge(av_mm, NQ * b + q + 1)
                for half in range(2):
                    copy(o_part(b, HI, half, q), av_part(half, q)).then_inc(o_hi, 1)

            def xph_split(b, q):
                act.wait_ge(xph_in[q], 16 * (b + 1))
                copy(xphase[:, HI, 4 * q:4 * q + 4, 1:P + 1],
                     xin[:, q * DIM:(q + 1) * DIM].rearrange("p (b j) -> p b j", b=4)).then_inc(xph_hi, 1)

            def y_context(b, with_front):
                act.wait_ge(y_mm, NQ * b + 1)
                if with_front:
                    act.wait_ge(c1_lo, 2 * (b + 2))
                    act.wait_ge(kv_lo, b + 2)
                else:
                    act.wait_ge(h_lo, 2 * b)
                for m in range(4):
                    last = act.activation(tmp[:, 0, m * P:(m + 1) * P], ybank[0][:, m * P:(m + 1) * P], ACT.Identity,
                                          bias=ctxb[:, bass.ds(b * GB + m, 1)])
                last.then_inc(y_t[0], 1)

            def y_split(b, q):
                act.wait_ge(yt_mm, NQ * b + q + 1)
                copy(y_part(HI, q), yt_view(q)).then_inc(y_hi, 1)

            def coef_exp(b):
                act.wait_ge(co_dve, CO * b + 4)
                act.activation(co[:, 3, :], co[:, 2, :], ACT.Exp,
                               scale=1.0 / (SEQ * 128.0 ** 0.5)).then_inc(co_exp, 1)

            def h_split(b, k):
                act.wait_ge(h_t, 2 * b + k + 1)
                copy(o_h[:, HI, 2 * k:2 * k + 2, :].rearrange("p a b -> p (a b)"),
                     tmp[:, k, :]).then_inc(h_hi, 1)

            def front_and_back(g):
                b = g - 1
                o_split(b, 0)
                o_split(b, 1)
                c1_split(g)
                kv_split(g)
                q_split(g, 0)
                xph_split(b, 0)
                xph_split(b, 1)
                q_split(g, 1)
                y_context(b, True)
                y_split(b, 0)
                y_split(b, 1)
                exp(g, 0)
                exp(g, 1)
                coef_exp(b)
                exp(g, 2)
                x_split(g + 1)
                probs_split(g, 0)
                h_split(b, 0)
                h_split(b, 1)
                probs_split(g, 1)
                exp(g, 3)
                probs_split(g, 2)
                probs_split(g, 3)

            def last_front_and_back(g):
                b = g - 1
                o_split(b, 0)
                o_split(b, 1)
                c1_split(g)
                kv_split(g)
                q_split(g, 0)
                xph_split(b, 0)
                xph_split(b, 1)
                q_split(g, 1)
                y_context(b, True)
                y_split(b, 0)
                y_split(b, 1)
                exp(g, 0)
                exp(g, 1)
                exp(g, 2)
                coef_exp(b)
                probs_split(g, 0)
                exp(g, 3)
                probs_split(g, 1)
                probs_split(g, 2)
                probs_split(g, 3)

            act.wait_ge(mlp_mm, 1)
            act.activation(hmlp[:, 0, :], small[:, 0:BATCH], ACT.Gelu, bias=st("b0")).then_inc(mlp_act, 1)
            act.wait_ge(kvc_in, 16)
            copy(wkv[:, HI], kv_in.unsqueeze(2).to_broadcast((P, PH, 4, 2 * HD)))
            copy(wconv[:, HI].rearrange("p a b -> p (a b)"), tmp[:, 0, 128:512]).then_inc(kvc_hi, 1)
            act.wait_ge(mlp_mm, 2)
            act.activation(hmlp[:, 1, :], small[:, 0:BATCH], ACT.Gelu, bias=st("b1")).then_inc(mlp_act, 1)
            split_weight(0)
            split_weight(1)
            x_split(0)
            split_weight(2)
            act.wait_ge(mixs_dve, 3)
            act.activation(mixs[0:BATCH, 8:8 + MIX], mixs[0:BATCH, 0:MIX], ACT.Exp).then_inc(mixs_exp, 1)
            for n in range(3, 6):
                split_weight(n)
            x_split(1)
            aggb_copy(0)
            split_weight(6)
            c1_split(0)
            for n in range(7, 10):
                split_weight(n)
            act.wait_ge(agg_outer, 4)
            kv_split(0)
            split_weight(10)
            q_split(0, 0)
            split_weight(11)
            q_split(0, 1)
            for c in range(1, 4):
                aggb_copy(c)
            for n in range(12, 17):
                split_weight(n)
            exp(0, 0)
            split_weight(18)
            exp(0, 1)
            exp(0, 2)
            split_weight(17)
            probs_split(0, 0)
            split_weight(19)
            probs_split(0, 1)
            exp(0, 3)
            probs_split(0, 2)
            probs_split(0, 3)

            with act.Fori(1, GROUPS - 1) as g:
                front_and_back(g)
            last_front_and_back(GROUPS - 1)
            b = GROUPS - 1
            o_split(b, 0)
            h_split(b - 1, 0)
            o_split(b, 1)
            h_split(b - 1, 1)
            xph_split(b, 0)
            xph_split(b, 1)
            y_context(b, False)
            y_split(b, 0)
            y_split(b, 1)
            coef_exp(b)
            h_split(b, 0)
            h_split(b, 1)

        @block.gpsimd
        def _(pool):
            def lo_of(out, whole, hi):
                return pool.tensor_tensor(out, whole, hi.bitcast(F32), ALU.subtract)

            pool.memset(kdiag[:].bitcast(F32).rearrange("p a b c -> p (a b c)"), 0.0).then_inc(zeroed, 1)
            pool.memset(vdiag[:].bitcast(F32).rearrange("p s b z c d -> p (s b z c d)"), 0.0).then_inc(zeroed, 1)
            pool.memset(xphase[:, :, :, 0:P + 2:P + 1].bitcast(F32), 0.0).then_inc(zeroed, 1)

            def split_weight(n):
                pool.wait_ge(w_hi, n + 1)
                pool.wait_ge(w_lo, n)
                w = W[WEIGHTS[n // PH]]
                lo_of(w[:, LO, n % PH, :], stage(n), w[:, HI, n % PH, :]).then_inc(w_lo, 1)

            def x_split(g, q):
                pool.wait_ge(x_hi, g + 1)
                sl = slice(q * DIM, (q + 1) * DIM)
                lo_of(x_of(g)[:, LO, sl], xin[:, sl], x_of(g)[:, HI, sl]).then_inc(x_lo, 1)

            def mix_product(g, products):
                for q in range(NQ):
                    last = pool.tensor_tensor(
                        products[:, q * 256:(q + 1) * 256].rearrange("p (o k) -> p o k", k=MIX),
                        mix_att[:, bass.ds(NQ * g + q, 1), :].to_broadcast((P, SEQ, MIX)),
                        keep_bank[:].rearrange("p (o k) -> p o k", k=MIX), ALU.mult)
                last.then_inc(mix_prod, 1)

            def mix_diag(g):
                pool.wait_ge(mix_split, 2 * (g + 1))
                pool.tensor_tensor(
                    mixd[:].rearrange("p s q m o -> p (s q) m o"),
                    mix_hl[:].bitcast(F32).rearrange("p s q o -> p (s q) o").unsqueeze(2)
                    .to_broadcast((P, 2 * NQ, 4, SEQ)),
                    kp("lane").unsqueeze(1).unsqueeze(3).to_broadcast((P, 2 * NQ, 4, SEQ)),
                    ALU.mult).then_inc(mix_ready, 1)

            def c1_split(g):
                for k in range(2):
                    pool.wait_ge(c1_hi, 2 * g + k + 1)
                    sl = [c1_y[:, s, 2 * k:2 * k + 2, :].rearrange("p a b -> p (a b)") for s in (HI, LO)]
                    lo_of(sl[LO], tmp[:, k, :], sl[HI]).then_inc(c1_lo, 1)

            def v_spread(g):
                pool.wait_ge(zeroed, 3)
                pool.wait_ge(v_tr, g + 1)
                pool.tensor_tensor(
                    vdiag[:, :, :, 0].rearrange("p s b c d -> p (s b) c d"),
                    vnat.rearrange("p (n e) -> p n e", e=2 * HD)[:, :, HD:2 * HD].unsqueeze(2)
                    .to_broadcast((P, 2 * GB, 4, HD)),
                    kp("quad").unsqueeze(1).unsqueeze(3).to_broadcast((P, 2 * GB, 4, HD)),
                    ALU.mult).then_inc(v_ready, 1)

            def heads(ap):
                return ap.rearrange("p (h k) -> p h k", k=SEQ)

            def s_subtract(g, p):
                pool.wait_ge(s_max, PAIRS * g + p + 1)
                s = heads(soft[:, p % 3, :])
                pool.tensor_tensor(s, s, smx[:, p, :].unsqueeze(2).to_broadcast((P, 2 * HC, SEQ)),
                                   ALU.subtract).then_inc(s_sub, 1)

            def probs_rest(g, p):
                pool.wait_ge(p_hi, PAIRS * g + p + 1)
                sl = [probsT[:, s, 2 * p:2 * p + 2].rearrange("p a b c -> p (a b c)") for s in (HI, LO)]
                lo_of(sl[LO], soft[:, 3 + p % 2, :], sl[HI]).then_inc(p_lo01, 1)

            def s_normalize(g, p):
                pool.wait_ge(s_rec, PAIRS * g + p + 1)
                s = heads(soft[:, p % 3, :])
                pool.tensor_tensor(s, s, srec[:, p, :].unsqueeze(2).to_broadcast((P, 2 * HC, SEQ)),
                                   ALU.mult).then_inc(s_norm, 1)

            pool.wait_ge(kvc_hi, 1)
            lo_of(wkv[:, LO], kv_in.unsqueeze(2).to_broadcast((P, PH, 4, 2 * HD)), wkv[:, HI])
            lo_of(wconv[:, LO].rearrange("p a b -> p (a b)"), tmp[:, 0, 128:512],
                  wconv[:, HI].rearrange("p a b -> p (a b)")).then_inc(kvc_lo, 1)
            x_split(0, 0)
            x_split(0, 1)
            pool.wait_ge(mixs_dve, 10)
            for c in range(4):
                pool.tensor_tensor(
                    aggb[:, c * DIM:(c + 1) * DIM].rearrange("p (q n) -> p q n", q=4),
                    attd[:, 4 * c:4 * c + 4].unsqueeze(2).to_broadcast((P, 4, P)),
                    st("bank_bias").unsqueeze(1).to_broadcast((P, 4, P)), ALU.mult).then_inc(agg_outer, 1)
                if c == 0:
                    pool.wait_ge(keep_in, 16)
                    mix_diag(0)
            x_split(1, 0)
            x_split(1, 1)
            v_spread(0)
            pool.wait_ge(kv_lo, 1)
            mix_product(1, tmp[:, 0, :])
            split_weight(12)
            mix_diag(1)
            s_subtract(0, 0)
            s_subtract(0, 1)
            s_normalize(0, 0)
            s_subtract(0, 2)
            s_normalize(0, 1)
            s_subtract(0, 3)
            probs_rest(0, 0)
            s_normalize(0, 2)
            s_normalize(0, 3)
            probs_rest(0, 1)
            split_weight(13)
            split_weight(14)
            split_weight(15)
            split_weight(16)

            def front_and_back(g):
                mix_product(g + 1, staging[:, 0, :])
                c1_split(g)
                v_spread(g)
                s_subtract(g, 0)
                s_subtract(g, 1)
                s_normalize(g, 0)
                mix_diag(g + 1)
                s_subtract(g, 2)
                s_normalize(g, 1)
                x_split(g + 1, 0)
                x_split(g + 1, 1)
                probs_rest(g, 0)
                s_subtract(g, 3)
                s_normalize(g, 2)
                probs_rest(g, 1)
                s_normalize(g, 3)

            def last_front_and_back(g):
                c1_split(g)
                v_spread(g)
                s_subtract(g, 0)
                s_subtract(g, 1)
                s_normalize(g, 0)
                s_subtract(g, 2)
                s_normalize(g, 1)
                s_subtract(g, 3)
                s_normalize(g, 2)
                s_normalize(g, 3)

            with pool.Fori(1, GROUPS - 1) as g:
                front_and_back(g)
            last_front_and_back(GROUPS - 1)

        @block.vector
        def _(dve):
            add, sub, mult = ALU.add, ALU.subtract, ALU.mult

            def heads(ap):
                return ap.rearrange("p (h k) -> p h k", k=SEQ)

            def split_weight(n, done=w_lo):
                dve.wait_ge(w_hi, n + 1)
                w = W[WEIGHTS[n // PH]]
                dve.tensor_tensor(w[:, LO, n % PH, :], stage(n), w[:, HI, n % PH, :].bitcast(F32), sub)\
                   .then_inc(done, 1)

            dve.wait_ge(start_in, 16)
            dve.tensor_copy(keep_bank[:], st("bank_w")).then_inc(bank_kept, 1)
            dve.wait_ge(ctx_mm, 1)
            dve.tensor_scalar(ctxb[:], sc[0][:, 0:BATCH], st("fside"), None, add).then_inc(ctx_done, 1)
            split_weight(0)
            split_weight(1)
            lg, B = mixs[0:BATCH], BATCH
            dve.wait_ge(mlp_mm, 3)
            dve.tensor_tensor(lg[:, 0:MIX], small[0:B, 0:MIX], st("b2")[0:B, :], add).then_inc(mixs_dve, 1)
            dve.wait_ge(mixs_dve, 1)
            dve.tensor_reduce(lg[:, 16:17], lg[:, 0:MIX], AX.X, ALU.max).then_inc(mixs_dve, 1)
            dve.wait_ge(mixs_dve, 2)
            dve.tensor_scalar(lg[:, 0:MIX], lg[:, 0:MIX], lg[:, 16:17], None, sub).then_inc(mixs_dve, 1)
            dve.wait_ge(mixs_exp, 1)
            dve.tensor_reduce(lg[:, 17:18], lg[:, 8:8 + MIX], AX.X, add).then_inc(mixs_dve, 1)
            dve.wait_ge(mixs_dve, 4)
            dve.reciprocal(lg[:, 18:19], lg[:, 17:18]).then_inc(mixs_dve, 1)
            dve.wait_ge(mixs_dve, 5)
            dve.tensor_scalar(lg[:, 0:MIX], lg[:, 8:8 + MIX], lg[:, 18:19], None, mult).then_inc(mixs_dve, 1)
            dve.wait_ge(mixs_dve, 6)
            dve.tensor_tensor(diag_att[0:B, :].rearrange("p (q k) -> p q k", k=MIX),
                              lg[:, 0:MIX].unsqueeze(1).to_broadcast((B, NB4, MIX)),
                              st("qmask")[0:B, :].unsqueeze(2).to_broadcast((B, NB4, MIX)), mult)\
               .then_inc(mixs_dve, 1)
            dve.wait_ge(mlp_mm, 4)
            dve.tensor_copy(mix_att[:], small[:, 0:NB4 * MIX].rearrange("p (q k) -> p q k", k=MIX))\
               .then_inc(mixs_dve, 1)
            dve.wait_ge(mixs_dve, 8)

            def mix_reduce(g, products):
                dve.wait_ge(mix_prod, g + 1)
                dve.tensor_reduce(mix_a[:].rearrange("p q o -> p (q o)"),
                                  products.rearrange("p (n k) -> p n k", k=MIX), AX.X, add)\
                   .then_inc(mix_red, 1)
                dve.wait_ge(mix_red, g + 1)
                if not (isinstance(g, int) and g == 0):
                    dve.wait_ge(c1_mm, 2 * g)
                dve.tensor_copy(mix_hl[:, HI], mix_a[:]).then_inc(mix_split, 1)
                dve.wait_ge(mix_split, 2 * g + 1)
                dve.tensor_tensor(mix_hl[:, LO], mix_a[:], mix_hl[:, HI].bitcast(F32), sub).then_inc(mix_split, 1)

            dve.wait_ge(bank_kept, 1)
            dve.tensor_tensor(diag_att.rearrange("p (q k) -> p q k", k=MIX), mix_att[:],
                              st("kdiag").unsqueeze(1).to_broadcast((P, NB4, MIX)), mult).then_inc(mixs_dve, 1)
            dve.wait_ge(mixs_dve, 9)
            dve.tensor_reduce(attd[:], diag_att.rearrange("p (q k) -> p q k", k=MIX), AX.X, add)\
               .then_inc(mixs_dve, 1)
            for q in range(NQ):
                last = dve.tensor_tensor(
                    soft[:, 1, q * 256:(q + 1) * 256].rearrange("p (o k) -> p o k", k=MIX),
                    mix_att[:, q:q + 1, :].to_broadcast((P, SEQ, MIX)),
                    keep_bank[:].rearrange("p (o k) -> p o k", k=MIX), mult)
            last.then_inc(mix_prod, 1)
            mix_reduce(0, soft[:, 1, :])
            for n in range(2, 7):
                split_weight(n)

            def c1_bias(g, first):
                for k in range(2):
                    if first:
                        dve.wait_ge(agg_done, 1)
                    dve.wait_ge(c1_mm, 2 * g + k + 1)
                    dve.tensor_tensor(tmp[:, k, :].rearrange("p (t n) -> p t n", t=2),
                                      feat[k].rearrange("p (t n) -> p t n", t=2),
                                      aggb[:, bass.ds(g * GT, GT)].unsqueeze(1).to_broadcast((P, 2, GT)), add)\
                       .then_inc(c1_t, 1)

            def kv(g):
                dve.wait_ge(kv_mm, g + 1)
                dve.tensor_scalar(kvt, small[:, 0:GT], kp("kvscale"), None, mult).then_inc(kv_t, 1)
                dve.wait_ge(kv_hi, g + 1)
                dve.tensor_tensor(kv_hl[:, LO, :], kvt, kv_hl[:, HI, :].bitcast(F32), sub).then_inc(kv_lo, 1)
                dve.wait_ge(kv_lo, g + 1)
                dve.transpose(vnat, kv_hl.bitcast(F32).rearrange("p s n -> p (s n)")).then_inc(v_tr, 1)

            def q_rest(g, k):
                dve.wait_ge(q_hi, 2 * g + k + 1)
                dve.tensor_tensor(q_half(LO, k), feat[k].rearrange("p (c b s) -> p b c s", c=2, b=GB),
                                  q_half(HI, k).bitcast(F32), sub).then_inc(q_lo, 1)

            def xph_rest(b, q):
                dve.wait_ge(xph_hi, NQ * b + q + 1)
                dve.tensor_tensor(xphase[:, LO, 4 * q:4 * q + 4, 1:P + 1],
                                  xin[:, q * DIM:(q + 1) * DIM].rearrange("p (b j) -> p b j", b=4),
                                  xphase[:, HI, 4 * q:4 * q + 4, 1:P + 1].bitcast(F32), sub).then_inc(xph_lo, 1)

            def h_rest(b, k):
                dve.wait_ge(h_hi, 2 * b + k + 1)
                sl = [o_h[:, s, 2 * k:2 * k + 2, :].rearrange("p a b -> p (a b)") for s in (HI, LO)]
                dve.tensor_tensor(sl[LO], tmp[:, k, :], sl[HI].bitcast(F32), sub).then_inc(h_lo, 1)

            def s_shifted(g, p, first):
                n = PAIRS * g + p
                dve.wait_ge(s_mm, n + 1)
                if p == 3:
                    dve.wait_ge(s_tr, n - 2)
                elif not first:
                    dve.wait_ge(s_tr, PAIRS * g)
                s = soft[:, p % 3, :]
                dve.tensor_tensor(s.rearrange("p (b n) -> p b n", b=2), sc[p % 2].rearrange("p (b n) -> p b n", b=2),
                                  kp("alibi").unsqueeze(1).to_broadcast((P, 2, GT)), add).then_inc(s_bias, 1)

            def s_maximum(g, p):
                dve.wait_ge(s_bias, PAIRS * g + p + 1)
                dve.tensor_reduce(smx[:, p, :], heads(soft[:, p % 3, :]), AX.X, ALU.max).then_inc(s_max, 1)

            def s_total(g, p):
                n = PAIRS * g + p
                dve.wait_ge(s_exp, n + 1)
                dve.tensor_reduce(ssum[:, p, :], heads(soft[:, p % 3, :]), AX.X, add).then_inc(s_sum, 1)
                dve.wait_ge(s_sum, n + 1)
                dve.reciprocal(srec[:, p, :], ssum[:, p, :]).then_inc(s_rec, 1)

            def s_transpose(g, p, first):
                n = PAIRS * g + p
                dve.wait_ge(s_norm, n + 1)
                if p < 2:
                    if not first:
                        dve.wait_ge(p_lo23, 2 * g + p - 1)
                else:
                    dve.wait_ge(p_lo01, 2 * g + p - 1)
                dve.transpose(soft[:, 3 + p % 2, :], soft[:, p % 3, :]).then_inc(s_tr, 1)

            def probs_rest(g, p):
                dve.wait_ge(p_hi, PAIRS * g + p + 1)
                sl = [probsT[:, s, 2 * p:2 * p + 2].rearrange("p a b c -> p (a b c)") for s in (HI, LO)]
                dve.tensor_tensor(sl[LO], soft[:, 3 + p % 2, :], sl[HI].bitcast(F32), sub)\
                   .then_inc(p_lo01 if p < 2 else p_lo23, 1)

            def o_rest(b, q):
                dve.wait_ge(o_hi, 2 * (NQ * b + q + 1))
                for half in range(2):
                    dve.tensor_tensor(o_part(b, LO, half, q), av_part(half, q),
                                      o_part(b, HI, half, q).bitcast(F32), sub).then_inc(o_lo, 1)

            def attn_residual(b, q):
                dve.wait_ge(x1_in[q], 16 * (b + 1))
                dve.wait_ge(wo_mm, NQ * b + q + 1)
                dve.tensor_tensor(x1_of(b)[:, q, :], attn_row(b, q), x1_of(b)[:, q, :], add).then_inc(x1_add, 1)

            def y_context(b, with_front):
                q = 1
                dve.wait_ge(y_mm, NQ * b + q + 1)
                if with_front:
                    dve.wait_ge(c1_lo, 2 * (b + 2))
                    dve.wait_ge(v_ready, b + 2)
                else:
                    dve.wait_ge(h_lo, 2 * b)
                dve.tensor_tensor(
                    tmp[:, q, :].rearrange("p (b j) -> p b j", b=4), ybank[q].rearrange("p (b j) -> p b j", b=4),
                    ctxb[:, bass.ds(b * GB + 4 * q, 4)].unsqueeze(2).to_broadcast((P, 4, P)), add)\
                   .then_inc(y_t[q], 1)

            def y_rest(b, q):
                dve.wait_ge(yt_mm, NQ * b + q + 1)
                dve.wait_ge(y_hi, NQ * b + q + 1)
                dve.tensor_tensor(y_part(LO, q), yt_view(q), y_part(HI, q).bitcast(F32), sub).then_inc(y_lo, 1)

            def y_total(b, q):
                dve.wait_ge(y_hi, NQ * b + q + 1)
                dve.tensor_reduce(ysum[:, :, 4 * q:4 * q + 4],
                                  ytbank[q].rearrange("p (b t o) -> p t b o", b=4, t=PH), AX.X, add)\
                   .then_inc(y_sum, 1)

            def coef_1(b):
                dve.wait_ge(y_sum, NQ * (b + 1))
                dve.tensor_tensor(expert_prod.rearrange("p (t b e) -> p t b e", t=PH, b=GB),
                                  ysum[:].unsqueeze(3).to_broadcast((P, PH, GB, EXPERTS)),
                                  expert_w[:].unsqueeze(2).to_broadcast((P, PH, GB, EXPERTS)), mult)\
                   .then_inc(co_dve, 1)
                dve.wait_ge(co_dve, CO * b + 1)
                dve.tensor_reduce(co[:, 0, :], expert_prod.rearrange("p (t n) -> p n t", t=PH), AX.X, add)\
                   .then_inc(co_dve, 1)

            def coef_2(b):
                lg = small[:, 0:GB * EXPERTS].rearrange("p (b e) -> p b e", e=EXPERTS)
                dve.wait_ge(co_mm, b + 1)
                dve.tensor_reduce(comx[:, 0, :], lg, AX.X, ALU.max).then_inc(co_dve, 1)
                dve.wait_ge(co_dve, CO * b + 3)
                dve.tensor_tensor(co[:, 2, :].rearrange("p (b e) -> p b e", e=EXPERTS), lg,
                                  comx[:, 0, :].unsqueeze(2).to_broadcast((P, GB, EXPERTS)), sub)\
                   .then_inc(co_dve, 1)

            def coef_3(b):
                ex = co[:, 3, :].rearrange("p (b e) -> p b e", e=EXPERTS)
                dve.wait_ge(co_exp, b + 1)
                dve.tensor_reduce(comx[:, 1, :], ex, AX.X, add).then_inc(co_dve, 1)
                dve.wait_ge(co_dve, CO * b + 5)
                dve.reciprocal(comx[:, 2, :], comx[:, 1, :]).then_inc(co_dve, 1)
                dve.wait_ge(co_dve, CO * b + 6)
                pairs = co[:, 3, :].rearrange("p (b c e) -> p c b e", c=EXPERTS // 2, e=2)
                for odd in range(2):
                    rws = slice(RANK * odd, RANK * (odd + 1))
                    dve.tensor_tensor(coef[rws], pairs[rws, :, :, odd],
                                      comx[rws, 2, :].unsqueeze(1).to_broadcast((RANK, EXPERTS // 2, GB)), mult)\
                       .then_inc(co_dve, 1)

            def hidden(b, k):
                dve.wait_ge(h_mm, 2 * b + k + 1)
                dve.wait_ge(co_dve, CO * (b + 1))
                dve.wait_ge(yt_mm, NQ * b + k + 1)
                dve.tensor_tensor(
                    tmp[:, k, :].rearrange("p (e s b) -> p e s b", s=SEQ, b=4),
                    feat[k].rearrange("p (e s b) -> p e s b", s=SEQ, b=4),
                    coef[:, 2 * k:2 * k + 2, :].rearrange("p e (q b) -> p (e q) b", b=4).unsqueeze(2)
                    .to_broadcast((P, 2 * NQ, SEQ, 4)), mult)\
                   .then_inc(h_t, 1)

            def out_residual(b, q):
                dve.wait_ge(out_mm, NQ * b + q + 1)
                dve.wait_ge(xph_in[q], 16 * (b + 1))
                dve.tensor_tensor(x1_of(b)[:, q, :], row[q], x1_of(b)[:, q, :], add).then_inc(out_add, 1)

            c1_bias(0, True)
            for k in range(2):
                dve.wait_ge(c1_hi, k + 1)
                sl = [c1_y[:, s, 2 * k:2 * k + 2, :].rearrange("p a b -> p (a b)") for s in (HI, LO)]
                dve.tensor_tensor(sl[LO], tmp[:, k, :], sl[HI].bitcast(F32), sub).then_inc(c1_lo, 1)
            for n in range(7, 10):
                split_weight(n)
            dve.wait_ge(expert_mm, 1)
            dve.tensor_copy(expert_w[:], row[0][:, 0:PH * EXPERTS].rearrange("p (t e) -> p t e", t=PH))\
               .then_inc(expert_done, 1)
            dve.wait_ge(keep_in, 16)
            kv(0)
            split_weight(10)
            q_rest(0, 0)
            split_weight(11)
            q_rest(0, 1)
            mix_reduce(1, tmp[:, 0, :])
            s_shifted(0, 0, True)
            s_maximum(0, 0)
            s_shifted(0, 1, True)
            s_maximum(0, 1)
            s_total(0, 0)
            s_shifted(0, 2, True)
            s_maximum(0, 2)
            s_total(0, 1)
            s_transpose(0, 0, True)
            s_shifted(0, 3, True)
            s_maximum(0, 3)
            s_transpose(0, 1, True)
            s_total(0, 2)
            s_total(0, 3)
            s_transpose(0, 2, True)
            split_weight(19, wu_lo)
            s_transpose(0, 3, True)
            probs_rest(0, 2)
            probs_rest(0, 3)
            split_weight(18, wu_lo)
            split_weight(17, wu_lo)
            dve.wait_ge(wu_lo, NW - LAST_LO)

            def front_and_back(g):
                b = g - 1
                o_rest(b, 0)
                c1_bias(g, False)
                o_rest(b, 1)
                attn_residual(b, 0)
                attn_residual(b, 1)
                kv(g)
                q_rest(g, 0)
                xph_rest(b, 0)
                mix_reduce(g + 1, staging[:, 0, :])
                xph_rest(b, 1)
                q_rest(g, 1)
                y_context(b, True)
                y_rest(b, 0)
                s_shifted(g, 0, False)
                y_total(b, 0)
                y_total(b, 1)
                s_maximum(g, 0)
                y_rest(b, 1)
                s_shifted(g, 1, False)
                coef_1(b)
                s_maximum(g, 1)
                s_total(g, 0)
                s_shifted(g, 2, False)
                s_maximum(g, 2)
                s_total(g, 1)
                coef_2(b)
                s_transpose(g, 0, False)
                coef_3(b)
                s_total(g, 2)
                hidden(b, 0)
                s_shifted(g, 3, False)
                h_rest(b, 0)
                hidden(b, 1)
                s_maximum(g, 3)
                s_transpose(g, 1, False)
                h_rest(b, 1)
                s_total(g, 3)
                out_residual(b, 0)
                s_transpose(g, 2, False)
                probs_rest(g, 2)
                s_transpose(g, 3, False)
                out_residual(b, 1)
                probs_rest(g, 3)

            def last_front_and_back(g):
                b = g - 1
                o_rest(b, 0)
                c1_bias(g, False)
                o_rest(b, 1)
                attn_residual(b, 0)
                attn_residual(b, 1)
                kv(g)
                q_rest(g, 0)
                xph_rest(b, 0)
                xph_rest(b, 1)
                q_rest(g, 1)
                y_context(b, True)
                y_rest(b, 0)
                s_shifted(g, 0, False)
                y_total(b, 0)
                s_maximum(g, 0)
                y_rest(b, 1)
                s_shifted(g, 1, False)
                y_total(b, 1)
                s_maximum(g, 1)
                s_total(g, 0)
                s_shifted(g, 2, False)
                s_maximum(g, 2)
                coef_1(b)
                s_total(g, 1)
                coef_2(b)
                s_transpose(g, 0, False)
                coef_3(b)
                s_shifted(g, 3, False)
                s_maximum(g, 3)
                probs_rest(g, 0)
                s_total(g, 2)
                s_transpose(g, 1, False)
                s_total(g, 3)
                s_transpose(g, 2, False)
                probs_rest(g, 1)
                s_transpose(g, 3, False)
                probs_rest(g, 2)
                probs_rest(g, 3)

            with dve.Fori(1, GROUPS - 1) as g:
                front_and_back(g)
            last_front_and_back(GROUPS - 1)
            b = GROUPS - 1
            hidden(b - 1, 0)
            o_rest(b, 0)
            o_rest(b, 1)
            hidden(b - 1, 1)
            h_rest(b - 1, 0)
            attn_residual(b, 0)
            attn_residual(b, 1)
            h_rest(b - 1, 1)
            out_residual(b - 1, 0)
            xph_rest(b, 0)
            out_residual(b - 1, 1)
            xph_rest(b, 1)
            y_context(b, False)
            y_rest(b, 0)
            y_rest(b, 1)
            y_total(b, 0)
            y_total(b, 1)
            coef_1(b)
            coef_2(b)
            coef_3(b)
            hidden(b, 0)
            h_rest(b, 0)
            hidden(b, 1)
            h_rest(b, 1)
            out_residual(b, 0)
            out_residual(b, 1)


def kernel(**inputs):
    import numpy as np
    import concourse.bacc as bacc
    from concourse.bass_utils import run_bass_kernel_spmd

    a = {k: np.asarray(v) for k, v in inputs.items()}
    f32 = np.float32
    J = DIM // PH

    def by_phase(rows):
        return rows.reshape(J, PH, -1)

    def cols_by_phase(m):
        return m.reshape(m.shape[0], J, PH).transpose(0, 2, 1).reshape(m.shape[0], DIM)

    def spread_rows(m, n=P):
        return np.broadcast_to(m.reshape(1, -1), (n, m.size))

    x = a["x"].reshape(BATCH // 4, 4, SEQ, DIM).transpose(0, 2, 1, 3).reshape(TOK, DIM)
    x = np.ascontiguousarray(cols_by_phase(x))

    wo = a["L0_attn_Wo"].reshape(4, 2, 4, HD, DIM).transpose(1, 0, 3, 2, 4)
    down = a["L0_ffn_lora_down"].transpose(1, 0, 2).reshape(DIM, EXPERTS * RANK)
    up = a["L0_ffn_lora_up"].reshape(PH, P, DIM).transpose(1, 0, 2)
    weights = {
        "wq": by_phase(a["L0_attn_Wq"]),
        "wo": cols_by_phase(np.ascontiguousarray(wo).reshape(-1, DIM)),
        "wd": by_phase(down),
        "worg": by_phase(cols_by_phase(np.ascontiguousarray(a["L0_ffn_W_org"].T))),
        "wu": cols_by_phase(np.ascontiguousarray(up).reshape(-1, DIM)),
    }
    weights = {k: np.ascontiguousarray(v.reshape(P, PH * DIM)) for k, v in weights.items()}

    conv_w = a["L0_cond2_weight"]
    width, taps = conv_w.shape[1], conv_w.shape[2]
    wconv = np.zeros((PH, SEQ, 3, PH, SEQ), f32)
    for r in range(PH):
        for tap in range(taps):
            m = r + tap - taps // 2
            for o in range(SEQ):
                i0 = o // width * width
                wconv[m % PH, i0:i0 + width, m // PH + 1, r, o] = conv_w[o, :, tap]
    kvc = np.concatenate([by_phase(a["L0_attn_Wkv"]).reshape(P, -1), wconv.reshape(P, -1)], axis=1)

    p = np.arange(P)
    first = 2.0 ** (-2.0 ** (-(np.log2(HEADS) - 3)))
    slopes = np.array([first ** (i + 1) for i in range(HEADS)], dtype=f32)
    pos = np.arange(SEQ)
    far = (pos[None, :] - pos[:, None]).astype(f32)
    alibi = slopes.reshape(4, 1, HC, 1) * far[None, :, None, :]
    alibi = np.where((far <= 0)[None, :, None, :], alibi, f32(-1e30)).astype(f32).reshape(P, HC * SEQ)
    kernels = a["L0_cond_weight"][..., 0]
    bank_bias = np.zeros((SEQ, 4, 4, SEQ), f32)
    for b in range(4):
        bank_bias[0:MIX, b, b, :] = a["L0_cond_bias_k"]

    sel = np.zeros((P, P), f32)
    sel[0:BATCH] = np.arange(BATCH)[:, None] % 4 == p[None, :] % 4
    qmask = np.zeros((P, BATCH // 4), f32)
    qmask[0:BATCH] = np.arange(BATCH)[:, None] // 4 == np.arange(BATCH // 4)[None, :]

    start = dict(
        sel=sel, qmask=qmask, condT=a["cond_128"].T, w0=a["L0_cond_W0"], w1=a["L0_cond_W1"], w2=a["L0_cond_W2"],
        b0=a["L0_cond_b0"].reshape(P, 1), b1=a["L0_cond_b1"].reshape(P, 1), b2=spread_rows(a["L0_cond_b2"]),
        bank_bias=bank_bias.reshape(P, P),
        bank_w=np.repeat(kernels.transpose(2, 1, 0).reshape(SEQ, SEQ * MIX), 4, axis=0),
        kdiag=(p[:, None] // 4 == np.arange(MIX)[None, :]).astype(f32),
        cwT=np.tile(a["L0_cond2_c_weight"].T, (1, PH)), fside=np.tile(a["fside_S_0"], PH).reshape(P, 1))
    keep = dict(
        alibi=alibi, kvscale=np.where(p % 32 < HD, HD ** -0.5, 1.0).astype(f32).reshape(P, 1),
        quad=(p[:, None] // 32 == np.arange(4)[None, :]).astype(f32),
        lane=(p[:, None] % 4 == np.arange(4)[None, :]).astype(f32),
        keysT=a["L0_ffn_lora_keys"].T,
        wq2=cols_by_phase(np.ascontiguousarray(a["L0_ffn_Wq"])), ones=np.ones((P, P), f32),
        ident=np.eye(P, dtype=f32))
    arrays = {
        "x": x,
        "start": np.concatenate([start[n] for n in START], axis=1),
        "keep": np.concatenate([keep[n] for n in KEEP], axis=1),
        "kvc": kvc, **weights,
    }
    arrays = {f"in_{k}": np.ascontiguousarray(v) for k, v in arrays.items()}

    nc = bacc.Bacc("TRN2", target_bir_lowering=False, num_devices=1)
    d = {k: nc.dram_tensor(k, v.shape, F32, kind="ExternalInput").ap() for k, v in arrays.items()}
    out = nc.dram_tensor("out", (TOK, DIM), F32, kind="ExternalOutput").ap()
    swap = nc.dram_tensor("swap", (NQ, PH, SEQ, 4, J), F32, kind="Internal").ap()
    build(nc, d["in_x"], d["in_start"], d["in_keep"], d["in_kvc"], {n: d[f"in_{n}"] for n in WEIGHTS}, swap, out)
    r = run_bass_kernel_spmd(nc, [arrays], core_ids=[0])
    got = r.results[0]["out"]
    got = got.reshape(BATCH // 4, SEQ, 4, PH, J).transpose(0, 2, 1, 4, 3)
    return np.ascontiguousarray(got).reshape(BATCH, SEQ, DIM)
```
